# Optimizing a Trainium2 kernel written in Bass

```python
import numpy as np
import jax
import jax.numpy as jnp

def _softmax(x, axis=-1):
    return jax.nn.softmax(x, axis=axis)

def _gelu(x):
    return jax.nn.gelu(x, approximate=True)

def _silu(x):
    return jax.nn.silu(x)

def _sigmoid(x):
    return jax.nn.sigmoid(x)

def _layernorm(x, axis=-1, eps=1e-05):
    m = jnp.mean(x, axis=axis, keepdims=True)
    v = jnp.var(x, axis=axis, keepdims=True)
    return (x - m) / jnp.sqrt(v + eps)

def _scatter_add(tgt, idx, src, axis=0):
    return tgt.at[idx].add(src)

def _segment_sum(src, seg, n):
    return jax.ops.segment_sum(src, seg, n)
kernel_name = 'mk_gnn_resnorm_d1_gnn_r8_f53b0b'

def setup_inputs(seed: int=0):
    np.random.seed(seed)
    _w = jnp.asarray

    def _rec_inputs():
        import jax
        import jax.numpy as jnp
        _gk = jax.random.key(seed)
        x = -0.0001006 + 1 * jax.random.normal(jax.random.fold_in(_gk, 1), (6250, 96), jnp.float32)
        src = jax.random.randint(jax.random.fold_in(_gk, 2), (200000,), 0, 6250, jnp.int32)
        dst = jnp.minimum((6250 * jax.random.uniform(jax.random.fold_in(_gk, 3), (200000,)) ** 2.0).astype(jnp.int32), 49999)
        _o = jnp.argsort(dst, stable=True)
        src = src[_o]
        dst = dst[_o]
        return (x, src, dst)
    x, src, dst = _rec_inputs()

    def _L0_gnn_setup():
        import jax, jax.numpy as jnp
        import numpy as np
        N_NODES = 6250
        N_EDGES = 100000
        D_MODEL = 96
        HEADS = 4
        key = jax.random.key(seed)
        ks = jax.random.split(key, 6)
        scale = 1.0 / np.sqrt(D_MODEL)
        return {'embeds': jax.random.normal(ks[0], (N_NODES, D_MODEL), dtype=jnp.float32), 'qW': jax.random.normal(ks[1], (D_MODEL, D_MODEL), dtype=jnp.float32) * scale, 'kW': jax.random.normal(ks[2], (D_MODEL, D_MODEL), dtype=jnp.float32) * scale, 'vW': jax.random.normal(ks[3], (D_MODEL, D_MODEL), dtype=jnp.float32) * scale, 'rows': jax.random.randint(ks[4], (N_EDGES,), 0, N_NODES, dtype=jnp.int32), 'cols': jax.random.randint(ks[5], (N_EDGES,), 0, N_NODES, dtype=jnp.int32)}
    _L0_gnn_all = _L0_gnn_setup()
    _L0_gnn_in = {k: v for k, v in _L0_gnn_all.items() if k in ('qW', 'kW', 'vW')}
    del _L0_gnn_all
    return {'x': x, 'src': src, 'dst': dst, 'L0_gnn_qW': _L0_gnn_in['qW'], 'L0_gnn_kW': _L0_gnn_in['kW'], 'L0_gnn_vW': _L0_gnn_in['vW']}

def reference(x, src, dst, L0_gnn_qW, L0_gnn_kW, L0_gnn_vW):
    import jax
    import jax.numpy as jnp

    def _L0_gnn_ref(embeds, qW, kW, vW, rows, cols):
        import jax, jax.numpy as jnp
        import numpy as np
        N_NODES = 6250
        N_EDGES = 100000
        D_MODEL = 96
        HEADS = 4
        nvar, d = embeds.shape
        dh = d // HEADS
        e = rows.shape[0]
        q = (embeds[rows] @ qW).reshape(e, HEADS, dh)
        k = (embeds[cols] @ kW).reshape(e, HEADS, dh)
        v = (embeds[cols] @ vW).reshape(e, HEADS, dh)
        scores = jnp.clip(jnp.einsum('ehd,ehd->eh', q, k), -10.0, 10.0)
        exp_s = jnp.exp(scores)
        norms = jax.ops.segment_sum(exp_s, rows, num_segments=nvar)[rows]
        w = exp_s / (norms + 1e-08)
        res = jax.ops.segment_sum(w[:, :, None] * v, rows, num_segments=nvar).reshape(nvar, d)
        return embeds + res
    x = _layernorm(x + _L0_gnn_ref(x, L0_gnn_qW, L0_gnn_kW, L0_gnn_vW, src, dst), axis=-1)
    return x

_drawn_inputs = setup_inputs


def setup_inputs(seed=0):
    import zlib

    import numpy as np

    out = dict(_drawn_inputs(seed))
    spreads = {}
    factors = {}
    for name, (base, spread) in spreads.items():
        noise = np.random.default_rng([zlib.crc32(name.encode()), seed]).standard_normal(out[name].shape)
        drawn = base * np.exp(spread * noise) if base else spread * noise
        out[name] = jnp.asarray(drawn.astype(out[name].dtype))
    for name, factor in factors.items():
        out[name] = (out[name] * factor).astype(out[name].dtype)
    return out
```

```python
from contextlib import ExitStack

import concourse.bass as bass
from concourse import mybir

ALU = mybir.AluOpType
ACT = mybir.ActivationFunctionType
AX = mybir.AxisListType
F32 = mybir.dt.float32
BF16 = mybir.dt.bfloat16
I32 = mybir.dt.int32
U32 = mybir.dt.uint32

P = 128
HEADS = 4
CLIP = 10.0
EPS_W = 1e-8
EPS_LN = 1e-5

ROWS_IT = 16
GROUP = 8
UNIT = 4
NPART = 2
BLK = 4
WROW = 196
TAG = 192


def gnn_program(nc, x, src, dst, wq, wk, wv, out):
    N, D = x.shape
    E = src.shape[0]
    DH = D // HEADS
    NT = -(-N // P)
    FULL_NT = N // P
    NREST = N - FULL_NT * P
    TRASH = NT
    NTAB = (NT + 1) * P
    EIT = ROWS_IT * P
    ITERS = -(-E // EIT)
    IPP = ITERS // NPART
    assert IPP * NPART == ITERS and ITERS <= P
    EFULL = E // EIT
    EREST = E - EFULL * EIT
    BPP_MIN = IPP * ROWS_IT // BLK + NT
    BPI = -(-BPP_MIN // IPP)
    BPP = BPI * IPP
    NBLK = NPART * BPP
    SORTED = NBLK * BLK * P
    GROUPS = ROWS_IT // GROUP
    UNITS = ROWS_IT // UNIT
    PAD_TILE = 64
    PAD_DST = N - 1
    FAR = 1 << 20
    assert SORTED < FAR and FULL_NT % 2 == 0 and NT == FULL_NT + 1 and FULL_NT % 2 == 0
    BYTES_BLK = BLK * P
    AW = D + HEADS

    kv3 = nc.dram_tensor("kv3_table", (NTAB, 3 * 2 * D), BF16).ap()
    kvf = nc.dram_tensor("kvf_table", (NTAB, 2 * D), F32).ap()
    rows_dram = nc.dram_tensor("sorted_rows", (SORTED, WROW), F32).ap()
    row_tmp = nc.dram_tensor("row_tmp", (ITERS, GROUPS), I32).ap()
    flag_tmp = nc.dram_tensor("flag_tmp", (ITERS, 1), F32).ap()

    with ExitStack() as ctx:
        def sb(name, shape, dt):
            return ctx.enter_context(nc.sbuf_tensor(name, shape, dt))

        def sem(name):
            return ctx.enter_context(nc.semaphore(name))

        def sems(name, n):
            return [sem(f"{name}{i}") for i in range(n)]

        ident_f = sb("ident_f", [P, P], F32)
        ident_b = sb("ident_b", [P, P], BF16)
        ones_b = sb("ones_b", [P, P], BF16)
        below_b = sb("below_b", [P, P], BF16)
        zeros_b = sb("zeros_b", [P, 3 * 2 * D], BF16)
        node_col = sb("node_col", [P, 2], F32)
        node_row = sb("node_row", [P, P], F32)
        tile_row = sb("tile_row", [P, NT, GROUP], BF16)
        pad_row = sb("pad_row", [P, BLK, WROW], F32)
        weights = sb("weights", [D, 3 * D], F32)
        q3 = sb("q3", [P, NT + 1, 3, D], BF16)
        acc = sb("acc", [P, NT + 1, AW], F32)
        src_tile = sb("src_tile", [P, ITERS, ROWS_IT], BF16)
        src_node = sb("src_node", [P, ITERS, ROWS_IT], F32)
        dst_col = sb("dst_col", [P, ITERS, ROWS_IT], I32)
        src_i = sb("src_i", [P, ITERS * ROWS_IT], I32)
        place = sb("place", [P, ITERS, ROWS_IT], I32)
        dst_local = sb("dst_local", [P, ROWS_IT, P], BF16)
        hits = sb("hits", [P, IPP, GROUPS, NT, GROUP], BF16)
        xT = sb("xT", [D, 2, P], F32)
        last3 = sb("last3", [P, 3, 3 * D], BF16)
        last_f = sb("last_f", [P, 2 * D], F32)
        window = sb("window", [P, GROUPS, 3, 2 * D], BF16)
        pick = sb("pick", [P, 2, UNIT * P], BF16)
        payload = sb("payload", [P, ROWS_IT, WROW], F32)
        place_now = sb("place_now", [P, ROWS_IT], U32)
        dst_now = sb("dst_now", [P, GROUP], U32)
        carry = sb("carry", [P, NT], F32)
        masked = sb("masked", [P, 2, NT, GROUP], F32)
        place_f = sb("place_f", [P, ITERS, ROWS_IT], F32)
        count = sb("count", [P, NT], F32)
        count_i = sb("count_i", [P, NT], I32)
        blocks_f = sb("blocks_f", [P, NT], F32)
        block_end = sb("block_end", [P, NPART, NT], F32)
        one_row = sb("one_row", [P, NT], F32)
        base = sb("base", [P, NT], F32)
        cmp_tile = sb("cmp_tile", [P, NT], F32)
        tile_of = sb("tile_of", [P, 2], F32)
        tail_i = sb("tail_i", [1, NPART * NT], I32)
        tile_i = sb("tile_i", [1, NBLK], I32)
        blk_iota = sb("blk_iota", [1, NBLK], F32)
        tile_f = sb("tile_f", [1, NPART, 2 * P], F32)
        start_i = sb("start_i", [1, NBLK], I32)
        span = sb("span", [P, 2, GROUPS], F32)
        over_f = sb("over_f", [P, 1], F32)
        span_i = sb("span_i", [P, GROUPS], I32)
        base_i = sb("base_i", [1, ITERS * GROUPS], I32)
        flags_f = sb("flags_f", [1, ITERS], F32)
        flag_f = sb("flag_f", [1, 1], F32)
        flag_i = sb("flag_i", [1, 1], I32)

        hits_words = hits[:].rearrange("p a b c d -> p (a b c d)").bitcast(F32)

        def carve(at, words):
            return hits_words[:, at:at + words]

        edge_i = carve(0, EIT).bitcast(I32)
        edge_f = carve(EIT, EIT)
        dest_i = carve(2 * EIT, EIT).bitcast(I32)
        dest_f = carve(3 * EIT, EIT)
        bits_i = place[:].rearrange("p i k -> p (i k)")
        y_all = carve(0, NT * D).rearrange("p (t d) -> p t d", d=D)
        x_all = carve(NT * D, NT * D).rearrange("p (t d) -> p t d", d=D)
        y2_all = carve(2 * NT * D, NT * D).rearrange("p (t d) -> p t d", d=D)
        stat = carve(3 * NT * D, 8 * NT).rearrange("p (k t) -> p k t", t=NT)
        inv = carve(3 * NT * D + 8 * NT, NT * HEADS).rearrange("p (t h) -> p t h", h=HEADS)

        def part_of(at, shape, dt):
            n = 1
            for d in shape:
                n *= d
            words = n // 2 if dt == BF16 else n
            v = carve(at, words)
            v = v.bitcast(BF16) if dt == BF16 else v
            dims = {f"d{i}": d for i, d in enumerate(shape)}
            names = " ".join(dims)
            return v.rearrange(f"p ({names}) -> p {names}", **dims), at + words

        x_in, at = part_of(4 * EIT, [2, D], F32)
        kv_f, at = part_of(at, [2, 2 * D], F32)
        parts3, at = part_of(at, [2, 3, 3 * D], BF16)
        rest, at = part_of(at, [2, 3 * D], F32)
        live_f = carve(4 * EIT, NBLK)[0:1]
        start_f = carve(4 * EIT + NBLK, NBLK)[0:1]

        blk, at = part_of(0, [BPI, BLK, WROW], F32)
        hot, at = part_of(at, [2, BLK, P], BF16)
        hot_f, at = part_of(at, [2, BLK, P], F32)
        hot_T, at = part_of(at, [2, BLK, P], BF16)
        qk, at = part_of(at, [2, BLK, D], F32)
        score, at = part_of(at, [2, BLK, HEADS], F32)
        clipped, at = part_of(at, [2, BLK, HEADS], F32)
        msg, at = part_of(at, [2, BLK, AW], F32)

        bank = [ctx.enter_context(nc.psum_tensor(f"bank{i}", [P, 512], F32)) for i in range(2)]
        kv_bank = [ctx.enter_context(nc.psum_tensor(f"kv_bank{i}", [P, 2, 512], F32)) for i in range(2)]
        q_bank = ctx.enter_context(nc.psum_tensor("q_bank", [P, 512], F32))
        ts_bank = ctx.enter_context(nc.psum_tensor("ts_bank", [P, 512], F32))
        turned = ts_bank[:, 0:BLK * P // 2].bitcast(BF16).rearrange("p (b n) -> p b n", b=BLK)
        sums = ts_bank[:, 384:384 + AW]
        picked_q = q_bank[:, 0:BLK * D].rearrange("p (b d) -> p b d", b=BLK)
        hist = q_bank[:, 0:NT * GROUP]
        totals = ts_bank[:, 0:NT]
        ranks = [b[:, 0:NT * GROUP] for b in bank]
        row_ps = ts_bank[0:1, 128:256]
        xT_ps = [b[0:D, 0:P] for b in bank]
        proj_ps = [b[:, 0, 0:3 * D] for b in kv_bank]
        turn_ps = [bank[0][:, 0:P], bank[1][:, 0:P]]

        consts = sem("consts")
        loads = sem("loads")
        edges_in = sem("edges_in")
        edge_pads = sem("edge_pads")
        x_loaded = sems("x_loaded", 2)
        xT_made = sems("xT_made", 2)
        xT_kept = sems("xT_kept", 2)
        proj_made = sems("proj_made", 2)
        high_made = sems("high_made", 2)
        low_made = sems("low_made", 2)
        dve_split = sem("dve_split")
        q_kept = sems("q_kept", 2)
        table_out = sems("table_out", 2)
        rest_out = sem("rest_out")
        dve_step = sem("dve_step")
        edges_split = sem("edges_split")
        turned_src = sem("turned_src")
        kept_src = sem("kept_src")
        span_made = sem("span_made")
        span_out = sem("span_out")
        base_in = sem("base_in")
        local_made = sem("local_made")
        flag_made = sem("flag_made")
        hits_made = sem("hits_made")
        hist_made = sem("hist_made")
        base_made = sem("base_made")
        carry_made = sem("carry_made")
        totals_made = sem("totals_made")
        ranks_made = sem("ranks_made")
        masked_made = sem("masked_made")
        rank_kept = sem("rank_kept")
        ends_made = sem("ends_made")
        tileof_made = sem("tileof_made")
        tilerow_made = sem("tilerow_made")
        tilerow_kept = sem("tilerow_kept")
        tables_made = sem("tables_made")
        place_made = sem("place_made")
        tails_out = sems("tails_out", NPART)
        window_in = sems("window_in", GROUPS)
        spread_rows = sems("spread_rows", UNITS)
        pick_made = sems("pick_made", UNITS)
        kv_made = sems("kv_made", UNITS)
        payload_made = sems("payload_made", UNITS)
        tags_made = sems("tags_made", GROUPS)
        scattered = sems("scattered", UNITS)
        slow_step = sem("slow_step")
        pool_turn = sem("pool_turn")
        blk_in = sems("blk_in", BPI)
        hot_made = sems("hot_made", BPI)
        turned_made = sems("turned_made", BPI)
        hotT_made = sems("hotT_made", BPI)
        hotf_made = sems("hotf_made", BPI)
        q_made = sems("q_made", BPI)
        qk_made = sems("qk_made", BPI)
        score_made = sems("score_made", BPI)
        clip_made = sems("clip_made", BPI)
        exp_made = sems("exp_made", BPI)
        msg_made = sems("msg_made", BPI)
        sum_made = sems("sum_made", BPI)
        acc_made = sems("acc_made", BPI)
        x_again = sem("x_again")
        fin = sem("fin")
        var_made = sem("var_made")
        dev_made = sem("dev_made")
        y_made = sem("y_made")
        stored = sem("stored")

        NCONST = 20

        def turn_before(k, n):
            if k >= 2:
                return k - 2, False
            return max(j for j in range(n) if j % 2 == k % 2), True

        def after(eng, sem_list, k, j, j1):
            eng.wait_ge(sem_list[k], j1)

        def slot_free(eng, sem_list, k, n, j, j1):
            prev, last_it = turn_before(k, n)
            eng.wait_ge(sem_list[prev], j if last_it else j1)

        def one_free(eng, sem_list, k, n, j, j1):
            eng.wait_ge(sem_list[k - 1 if k else n - 1], j1 if k else j)

        block = ctx.enter_context(nc.Block())

        @block.gpsimd
        def _(pool):
            pool.memset(ident_f[:], 0.0).then_inc(consts, 1)
            pool.memset(ident_b[:], 0.0).then_inc(consts, 1)
            pool.memset(below_b[:], 1.0).then_inc(consts, 1)
            pool.wait_ge(consts, 3)
            for m in (ident_f, ident_b):
                pool.affine_select(out=m[:], in_=m[:], compare_op=ALU.not_equal, fill=1.0, base=0,
                                   pattern=[[-1, P]], channel_multiplier=1).then_inc(consts, 1)
            pool.affine_select(out=below_b[:], in_=below_b[:], compare_op=ALU.is_gt, fill=0.0, base=0,
                               pattern=[[1, P]], channel_multiplier=-1).then_inc(consts, 1)
            pool.memset(pad_row[:], 0.0).then_inc(consts, 1)
            pool.wait_ge(consts, 7)
            pool.memset(pad_row[:, :, TAG:TAG + 1], -1.0).then_inc(consts, 1)
            pool.memset(ones_b[:], 1.0).then_inc(consts, 1)
            pool.memset(zeros_b[:], 0.0).then_inc(consts, 1)
            pool.memset(one_row[:], 1.0).then_inc(consts, 1)
            pool.memset(q3[:, FULL_NT:NT + 1], 0.0).then_inc(consts, 1)
            pool.memset(last3[:], 0.0).then_inc(consts, 1)
            pool.memset(last_f[:], 0.0).then_inc(consts, 1)
            pool.memset(acc[:], 0.0).then_inc(consts, 1)
            pool.memset(payload[:, :, TAG:WROW], 0.0).then_inc(consts, 1)
            for held, pattern, by in ((node_col, [[P, 2]], 1), (node_row, [[1, P]], 0),
                                      (tile_row, [[1, NT], [0, GROUP]], 0), (blk_iota, [[1, NBLK]], 0)):
                pool.iota(held[:], pattern, base=0, channel_multiplier=by,
                          allow_small_or_imprecise_dtypes=True).then_inc(consts, 1)

            pool.wait_ge(place_made, 1)
            pool.wait_ge(flag_made, 1)
            over = pool.value_load(flag_i[0:1, 0:1], min_val=0, max_val=1)

            for s in range(2):
                pool.wait_ge(table_out[s], 32 * (FULL_NT // 2))
            pool.wait_ge(rest_out, 64)
            last_place = pool.to_reg(SORTED - 1)
            last_row = pool.to_reg(NTAB - 1)

            def scatter(u, it1):
                pool.wait_ge(payload_made[u], it1)
                pool.sem_inc(pool_turn, 1)
                for k in range(UNIT * u, UNIT * (u + 1)):
                    pool.indirect_dma_start(
                        out=rows_dram, out_offset=bass.IndirectOffsetOnAxis(ap=place_now[:, k:k + 1], axis=0),
                        in_=payload[:, k, :], in_offset=None,
                        bounds_check=last_place, oob_is_err=False).then_inc(scattered[u], 16)

            def fast_part(part):
                pool.wait_ge(tails_out[part], 16 * NT)
                with pool.Fori(part * IPP, (part + 1) * IPP) as it:
                    it1 = pool.snap(it + 1)
                    it2 = pool.snap(it * 2 + 2)
                    for u in range(UNITS):
                        if u % (UNITS // GROUPS) == 0:
                            pool.wait_ge(tags_made[u // (UNITS // GROUPS)], it2)
                        scatter(u, it1)

            STEPS = 1 + 16 * GROUP

            def slow_part(part):
                pool.wait_ge(tails_out[part], 16 * NT)
                with pool.Fori(part * IPP, (part + 1) * IPP) as it:
                    it1 = pool.snap(it + 1)
                    it2 = pool.snap(it * 2 + 2)
                    copied = [pool.snap(it * (GROUPS * STEPS) + (g * STEPS + 1)) for g in range(GROUPS)]
                    gathered = [pool.snap(it * (GROUPS * STEPS) + (g + 1) * STEPS) for g in range(GROUPS)]
                    for g in range(GROUPS):
                        for u in range(2 * g, 2 * g + 2):
                            pool.wait_ge(payload_made[u], it1)
                        pool.wait_ge(tags_made[g], it2)
                        pool.tensor_copy(dst_now[:], dst_col[:, bass.ds(it, 1), g * GROUP:(g + 1) * GROUP]
                                         .rearrange("p a b -> p (a b)")).then_inc(slow_step, 1)
                        pool.wait_ge(slow_step, copied[g])
                        pool.sem_inc(pool_turn, 1)
                        for k in range(GROUP):
                            pool.indirect_dma_start(
                                out=payload[:, g * GROUP + k, 0:2 * D], out_offset=None,
                                in_=kvf, in_offset=bass.IndirectOffsetOnAxis(ap=dst_now[:, k:k + 1], axis=0),
                                bounds_check=last_row, oob_is_err=False).then_inc(slow_step, 16)
                        pool.wait_ge(slow_step, gathered[g])
                        for u in range(2 * g, 2 * g + 2):
                            scatter(u, it1)

            with pool.If(over == 0):
                for part in range(NPART):
                    fast_part(part)
            with pool.Else():
                for part in range(NPART):
                    slow_part(part)

        @block.sync
        def _(sp):
            sp.dma_start(weights[:, 0:D], wk).then_inc(loads, 16)
            sp.dma_start(weights[:, D:2 * D], wv).then_inc(loads, 16)
            sp.dma_start(weights[:, 2 * D:3 * D], wq).then_inc(loads, 16)
            sp.wait_ge(edge_pads, 2)
            for flat, held in ((src, edge_i), (dst, dest_i)):
                sp.dma_start(held[0:EFULL, :], flat[0:EFULL * EIT].rearrange("(i e) -> i e", e=EIT)
                             ).then_inc(edges_in, 16)
                sp.dma_start(held[EFULL:EFULL + 1, 0:EREST],
                             flat[EFULL * EIT:E].rearrange("(i e) -> i e", i=1)).then_inc(edges_in, 16)

            with sp.Fori(0, FULL_NT // 2) as j:
                for s in range(2):
                    sp.wait_ge(xT_made[s], j)
                    sp.dma_start(x_in[:, s, :], x[bass.ds((2 * j + s) * P, P), :]).then_inc(x_loaded[s], 16)
            sp.wait_ge(xT_made[0], FULL_NT // 2)
            sp.dma_start(x_in[0:NREST, 0, :], x[FULL_NT * P:N, :]).then_inc(x_loaded[0], 16)

            sp.wait_ge(span_made, 1)
            sp.dma_start(row_tmp, span_i[0:ITERS, :]).then_inc(span_out, 16)
            sp.dma_start(flag_tmp, over_f[0:ITERS, :]).then_inc(span_out, 16)
            sp.wait_ge(span_out, 32)
            sp.dma_start(base_i[:], row_tmp.rearrange("(o a) b -> o (a b)", o=1)).then_inc(base_in, 16)
            sp.dma_start(flags_f[:], flag_tmp.rearrange("(o a) b -> o (a b)", o=1)).then_inc(base_in, 16)

            rows_of_block = rows_dram.rearrange("(b p k) w -> b p k w", p=P, k=BLK)
            sp.wait_ge(tables_made, 1)
            sp.wait_ge(consts, NCONST)
            for part in range(NPART):
                with sp.Fori(part * NT, (part + 1) * NT) as t:
                    b = sp.value_load(tail_i[0:1, bass.ds(t, 1)], min_val=0, max_val=NBLK - 1)
                    sp.dma_start(rows_of_block[bass.ds(b, 1)].rearrange("b p k w -> (b p) k w"),
                                 pad_row[:]).then_inc(tails_out[part], 16)

            for s in range(2):
                sp.wait_ge(table_out[s], 32 * (FULL_NT // 2))
            sp.wait_ge(rest_out, 64)
            sp.wait_ge(base_in, 32)
            with sp.Fori(0, ITERS) as it:
                it2 = sp.snap(it * GROUPS)
                for g in range(GROUPS):
                    sp.wait_ge(kv_made[2 * g + 1], it)
                    lo = sp.value_load(base_i[0:1, bass.ds(it2 + g, 1)], min_val=0, max_val=N - 1)
                    sp.dma_start(window[:, g].rearrange("p a b -> p (a b)"),
                                 kv3[bass.ds(lo, P), :]).then_inc(window_in[g], 16)

            for part in range(NPART):
                for u in range(UNITS):
                    sp.wait_ge(scattered[u], 16 * UNIT * IPP * (part + 1))
                with sp.Fori(part * IPP, (part + 1) * IPP) as j:
                    j5 = sp.snap(j * BPI)
                    for k in range(BPI):
                        b = sp.value_load(start_i[0:1, bass.ds(j5 + k, 1)], min_val=0, max_val=NBLK - 1)
                        sp.wait_ge(msg_made[k], j)
                        sp.dma_start(blk[:, k], rows_of_block[bass.ds(b, 1)].rearrange("b p k w -> (b p) k w")
                                     ).then_inc(blk_in[k], 16)

            for k in range(BPI):
                sp.wait_ge(acc_made[k], ITERS)
            sp.dma_start(x_all[:, 0:FULL_NT, :], x[0:FULL_NT * P, :].rearrange("(t p) d -> p t d", p=P)
                         ).then_inc(x_again, 16)
            sp.dma_start(x_all[0:NREST, FULL_NT, :], x[FULL_NT * P:N, :]).then_inc(x_again, 16)
            sp.wait_ge(y_made, 1)
            sp.dma_start(out[0:FULL_NT * P, :].rearrange("(t p) d -> p t d", p=P), y_all[:, 0:FULL_NT, :]
                         ).then_inc(stored, 16)
            sp.dma_start(out[FULL_NT * P:N, :], y_all[0:NREST, FULL_NT, :]).then_inc(stored, 16)
            sp.wait_ge(stored, 32)

        @block.scalar
        def _(act):
            def tables(s, j1, n, full, parts, q_to):
                act.wait_ge(xT_made[s], j1)
                act.activation(xT[:, s, 0:n], xT_ps[s][:, 0:n], ACT.Copy).then_inc(xT_kept[s], 1)
                act.wait_ge(proj_made[s], j1)
                act.activation(full, proj_ps[s][0:n, 0:2 * D], ACT.Copy).then_inc(high_made[s], 1)
                act.activation(parts[:, 0, :], proj_ps[s][0:n, :], ACT.Copy).then_inc(high_made[s], 1)
                act.wait_ge(low_made[s], j1)
                act.activation(q_to, parts[:, :, 2 * D:3 * D], ACT.Copy).then_inc(q_kept[s], 1)

            act.wait_ge(consts, NCONST)
            with act.Fori(0, FULL_NT // 2) as j:
                j1 = act.snap(j + 1)
                for s in range(2):
                    act.wait_ge(table_out[s], j * 32)
                    tables(s, j1, P, kv_f[:, s, :], parts3[:, s],
                           q3[:, bass.ds(2 * j + s, 1), :, :].rearrange("p o a d -> p (o a) d"))
                    act.wait_ge(q_kept[s], j1)
                    rows = bass.ds((2 * j + s) * P, P)
                    act.dma_start(kv3[rows, :].rearrange("p (a b) -> p a b", a=3),
                                  parts3[:, s, :, 0:2 * D]).then_inc(table_out[s], 16)
                    act.dma_start(kvf[rows, :], kv_f[:, s, :]).then_inc(table_out[s], 16)
            tables(0, FULL_NT // 2 + 1, NREST, last_f[0:NREST, :], last3[0:NREST], q3[0:NREST, FULL_NT])
            act.wait_ge(q_kept[0], FULL_NT // 2 + 1)
            at = FULL_NT * P
            act.dma_start(kv3[at:at + P, :].rearrange("p (a b) -> p a b", a=3), last3[:, :, 0:2 * D]
                          ).then_inc(rest_out, 16)
            act.dma_start(kvf[at:at + P, :], last_f[:]).then_inc(rest_out, 16)
            act.dma_start(kv3[at + P:at + 2 * P, :], zeros_b[:]).then_inc(rest_out, 16)
            act.dma_start(kvf[at + P:at + 2 * P, :], zeros_b[:, 0:4 * D].bitcast(F32)).then_inc(rest_out, 16)

            for part in range(NPART):
                with act.Fori(part * 2 * IPP, (part + 1) * 2 * IPP) as b:
                    act.wait_ge(totals_made, b + (part + 1))
                    act.activation(carry[:], totals, ACT.Copy).then_inc(carry_made, 1)

            act.wait_ge(place_made, 1)
            act.wait_ge(consts, NCONST)
            with act.Fori(0, ITERS) as it:
                it1 = act.snap(it + 1)
                it64 = act.snap(it * (16 * UNIT))
                here = bass.ds(it, 1)
                for u in range(UNITS):
                    if u % 2 == 0:
                        g = u // 2
                        cols = slice(g * GROUP, (g + 1) * GROUP)
                        act.wait_ge(scattered[u], it64)
                        act.wait_ge(scattered[u + 1], it64)
                        act.activation(place_now[:, cols],
                                       place[:, here, cols].rearrange("p a b -> p (a b)"), ACT.Copy
                                       ).then_inc(tags_made[g], 1)
                        act.activation(payload[:, cols, TAG:TAG + 1].rearrange("p a b -> p (a b)"),
                                       src_node[:, here, cols].rearrange("p a b -> p (a b)"),
                                       ACT.Copy).then_inc(tags_made[g], 1)
                    act.wait_ge(kv_made[u], it1)
                    act.activation(payload[:, UNIT * u:UNIT * (u + 1), 0:2 * D]
                                   .rearrange("p (a b) d -> p a b d", a=2),
                                   kv_bank[u % 2][:, :, 0:4 * D].rearrange("p a (b d) -> p a b d", b=2),
                                   ACT.Copy).then_inc(payload_made[u], 1)

            with act.Fori(0, ITERS) as j:
                j1 = act.snap(j + 1)
                for s in range(BPI + 1):
                    if s < BPI:
                        k = s
                        slot_free(act, sum_made, k, BPI, j, j1)
                        after(act, hot_made, k, j, j1)
                        act.activation(hot_f[:, k % 2], hot[:, k % 2], ACT.Copy).then_inc(hotf_made[k], 1)
                        slot_free(act, q_made, k, BPI, j, j1)
                        after(act, turned_made, k, j, j1)
                        act.activation(hot_T[:, k % 2], turned, ACT.Copy).then_inc(hotT_made[k], 1)
                    if s >= 1:
                        k = s - 1
                        slot_free(act, sum_made, k, BPI, j, j1)
                        after(act, clip_made, k, j, j1)
                        act.activation(msg[:, k % 2, :, D:AW], clipped[:, k % 2], ACT.Exp
                                       ).then_inc(exp_made[k], 1)

            act.wait_ge(var_made, 1)
            act.activation(stat[:, 3, :], stat[:, 2, :], ACT.Sqrt).then_inc(dev_made, 1)

        @block.tensor
        def _(pe):
            pe.wait_ge(consts, NCONST)
            pe.wait_ge(loads, 48)

            def tables(s, j, j1, n):
                pe.wait_ge(x_loaded[s], j1 * 16)
                pe.wait_ge(xT_kept[s], j)
                pe.transpose(xT_ps[s][:, 0:n], x_in[0:n, s, :], ident_f[0:n, 0:n]).then_inc(xT_made[s], 1)

            def project(s, j, j1, n):
                pe.wait_ge(xT_kept[s], j1)
                pe.wait_ge(low_made[s], j)
                pe.matmul(proj_ps[s][0:n, :], xT[:, s, 0:n], weights[:], start=True, stop=True
                          ).then_inc(proj_made[s], 1)

            with pe.Fori(0, FULL_NT // 2) as j:
                j1 = pe.snap(j + 1)
                for s in range(2):
                    tables(s, j, j1, P)
                for s in range(2):
                    project(s, j, j1, P)
            tables(0, FULL_NT // 2, FULL_NT // 2 + 1, NREST)
            project(0, FULL_NT // 2, FULL_NT // 2 + 1, NREST)

            pe.wait_ge(edges_split, 2)
            pe.wait_ge(xT_kept[0], FULL_NT // 2 + 1)
            pe.wait_ge(xT_kept[1], FULL_NT // 2)
            pe.wait_ge(low_made[0], FULL_NT // 2 + 1)
            for n in range(2 * ROWS_IT):
                held, k = (edge_f, dest_f)[n // ROWS_IT], n % ROWS_IT
                if n >= 2:
                    pe.wait_ge(kept_src, n - 1)
                pe.transpose(turn_ps[n % 2][:, 0:ITERS], held[0:ITERS, k * P:(k + 1) * P],
                             ident_f[0:ITERS, 0:ITERS]).then_inc(turned_src, 1)
            pe.wait_ge(kept_src, 2 * ROWS_IT)

            for part in range(NPART):
                if part:
                    pe.wait_ge(tilerow_kept, 2 * part)
                pe.matmul(hist, ones_b[:], zeros_b[:, 0:NT * GROUP], start=True, stop=False)
                with pe.Fori(0, IPP) as i:
                    pe.wait_ge(hits_made, i + (part * IPP + 1))
                    for h in range(GROUPS):
                        pe.matmul(hist, ones_b[:], hits[:, bass.ds(i, 1), h].rearrange("p a t c -> p (a t c)"),
                                  start=False, stop=False)
                pe.matmul(hist, ones_b[:], zeros_b[:, 0:NT * GROUP], start=False, stop=True
                          ).then_inc(hist_made, 1)
                for h in range(2):
                    pe.wait_ge(tileof_made, 2 * part + h + 1)
                    if 2 * part + h:
                        pe.wait_ge(tilerow_kept, 2 * part + h)
                    pe.matmul(row_ps, tile_of[:, h:h + 1], ident_f[:], start=True, stop=True
                              ).then_inc(tilerow_made, 1)
                pe.wait_ge(base_made, part + 1)
                pe.wait_ge(tilerow_kept, 2 * part + 2)
                pe.matmul(totals, ident_f[:], base[:], start=True, stop=False, skip_group_check=True
                          ).then_inc(totals_made, 1)
                with pe.Fori(0, IPP) as i:
                    for h in range(GROUPS):
                        now = hits[:, bass.ds(i, 1), h].rearrange("p a t c -> p (a t) c")
                        to = ranks[h].rearrange("p (t c) -> p t c", c=GROUP)
                        pe.wait_ge(masked_made, i * 2 + (2 * part * IPP - 1 + h) if part or h else i * 2)
                        pe.matmul(to, below_b[:], now, start=True, stop=False)
                        for c in range(GROUP - 1):
                            pe.matmul(to[:, :, c + 1:], ones_b[:],
                                      now[:, :, c:c + 1].to_broadcast([P, NT, GROUP - 1 - c]),
                                      start=False, stop=False)
                        pe.wait_ge(carry_made, i * 2 + (2 * part * IPP + h + 1))
                        pe.matmul(to, ident_f[:], carry[:].unsqueeze(2).to_broadcast([P, NT, GROUP]),
                                  start=False, stop=True).then_inc(ranks_made, 1)
                        for c in range(GROUP):
                            mm = pe.matmul(totals, ones_b[:],
                                           now[:, :, c:c + 1].rearrange("p t c -> p (t c)"),
                                           start=False, stop=False, skip_group_check=True)
                        mm.then_inc(totals_made, 1)

            pe.wait_ge(local_made, GROUPS)
            pe.wait_ge(place_made, 1)
            with pe.Fori(0, ITERS) as it:
                it1 = pe.snap(it + 1)
                it16 = pe.snap(it * 16 + 16)
                sel = ident_b[0:ITERS, bass.ds(it, 1)].to_broadcast([ITERS, P])
                for s in range(UNITS + 1):
                    if s < UNITS:
                        u = s
                        slot_free(pe, pick_made, u, UNITS, it, it1)
                        pe.matmul(bank[u % 2][:], sel,
                                  dst_local[0:ITERS, UNIT * u:UNIT * (u + 1), :].rearrange("p a b -> p (a b)"),
                                  start=True, stop=True).then_inc(spread_rows[u], 1)
                    if s >= 1:
                        u = s - 1
                        after(pe, pick_made, u, it, it1)
                        slot_free(pe, payload_made, u, UNITS, it, it1)
                        if u % 2 == 0:
                            pe.wait_ge(window_in[u // 2], it16)
                        for k in range(UNIT):
                            to = kv_bank[u % 2][:, k // 2, (k % 2) * 2 * D:(k % 2 + 1) * 2 * D]
                            for a in range(3):
                                mm = pe.matmul(to, pick[:, u % 2, k * P:(k + 1) * P], window[:, u // 2, a, :],
                                               start=(a == 0), stop=(a == 2))
                        mm.then_inc(kv_made[u], 1)

            with pe.Fori(0, ITERS) as j:
                j1 = pe.snap(j + 1)
                j5 = pe.snap(j * BPI)
                for s in range(BPI + 2):
                    if s < BPI:
                        k = s
                        after(pe, hot_made, k, j, j1)
                        one_free(pe, hotT_made, k, BPI, j, j1)
                        for b in range(BLK):
                            mm = pe.transpose(turned[:, b, :], hot[:, k % 2, b, :], ident_b[:])
                        mm.then_inc(turned_made[k], 1)
                    if 1 <= s <= BPI:
                        k = s - 1
                        tile = pe.value_load(tile_i[0:1, bass.ds(j5 + k, 1)], min_val=0, max_val=NT)
                        after(pe, hotT_made, k, j, j1)
                        one_free(pe, qk_made, k, BPI, j, j1)
                        for b in range(BLK):
                            for a in range(3):
                                mm = pe.matmul(picked_q[:, b, :], hot_T[:, k % 2, b, :],
                                               q3[:, bass.ds(tile, 1), a, :].rearrange("p a d -> p (a d)"),
                                               start=(a == 0), stop=(a == 2))
                        mm.then_inc(q_made[k], 1)
                    if s >= 2:
                        k = s - 2
                        after(pe, msg_made, k, j, j1)
                        after(pe, hotf_made, k, j, j1)
                        one_free(pe, acc_made, k, BPI, j, j1)
                        for b in range(BLK):
                            mm = pe.matmul(sums, hot_f[:, k % 2, b, :], msg[:, k % 2, b, :],
                                           start=(b == 0), stop=(b == BLK - 1))
                        mm.then_inc(sum_made[k], 1)

        @block.vector
        def _(dve):
            step = [0]

            def link(ins):
                step[0] += 1
                ins.then_inc(dve_step, 1)
                dve.wait_ge(dve_step, step[0])

            dve.memset(edge_i[:, :], PAD_TILE * P).then_inc(edge_pads, 1)
            dve.memset(dest_i[:, :], PAD_DST).then_inc(edge_pads, 1)
            dve.wait_ge(edges_in, 64)
            dve.tensor_copy(edge_f[0:ITERS], edge_i[0:ITERS]).then_inc(edges_split, 1)
            dve.tensor_copy(dest_f[0:ITERS], dest_i[0:ITERS]).then_inc(edges_split, 1)
            dve.wait_ge(edges_split, 2)
            grouped = dest_f[0:ITERS].rearrange("p (g e) -> p g e", g=GROUPS)
            link(dve.tensor_reduce(span[0:ITERS, 0, :], grouped, AX.X, ALU.min))
            link(dve.tensor_reduce(span[0:ITERS, 1, :], grouped, AX.X, ALU.max))
            link(dve.tensor_copy(span_i[0:ITERS, :], span[0:ITERS, 0, :]))
            link(dve.tensor_tensor(span[0:ITERS, 1, :], span[0:ITERS, 1, :], span[0:ITERS, 0, :], ALU.subtract))
            dve.tensor_reduce(over_f[0:ITERS, :], span[0:ITERS, 1, :], AX.X, ALU.max).then_inc(span_made, 1)
            for g in range(GROUPS):
                cols = slice(g * GROUP * P, (g + 1) * GROUP * P)
                ins = dve.tensor_scalar(dst_local[0:ITERS, g * GROUP:(g + 1) * GROUP, :]
                                        .rearrange("p a b -> p (a b)"),
                                        dest_f[0:ITERS, cols], span[0:ITERS, 0, g:g + 1], None, ALU.subtract)
                ins.then_inc(local_made, 1)

            def split(s, j1, j2, n, parts, base):
                dve.wait_ge(proj_made[s], j1)
                dve.wait_ge(high_made[s], j2)
                dve.tensor_tensor(rest[0:n, s, :], proj_ps[s][0:n, :], parts[:, 0, :], ALU.subtract
                                  ).then_inc(dve_split, 1)
                dve.wait_ge(dve_split, base + 1)
                dve.tensor_copy(parts[:, 1, :], rest[0:n, s, :]).then_inc(dve_split, 1)
                dve.wait_ge(dve_split, base + 2)
                dve.tensor_tensor(parts[:, 2, :], rest[0:n, s, :], parts[:, 1, :], ALU.subtract
                                  ).then_inc(low_made[s], 1)

            dve.wait_ge(consts, NCONST)
            with dve.Fori(0, FULL_NT // 2) as j:
                j1 = dve.snap(j + 1)
                j2 = dve.snap(j * 2 + 2)
                j4 = dve.snap(j * 4)
                for s in range(2):
                    split(s, j1, j2, P, parts3[:, s], j4 + 2 * s)
            split(0, FULL_NT // 2 + 1, FULL_NT + 2, NREST, last3[0:NREST], 2 * FULL_NT)

            for n in range(2 * ROWS_IT):
                to, k = (src_i[:].rearrange("p (i k) -> p i k", k=ROWS_IT), dst_col[:])[n // ROWS_IT], n % ROWS_IT
                dve.wait_ge(turned_src, n + 1)
                ins = dve.tensor_copy(to[:, :, k], turn_ps[n % 2][:, 0:ITERS])
                ins.then_inc(kept_src, 1)
            dve.wait_ge(kept_src, 2 * ROWS_IT)
            for s in range(2):
                dve.wait_ge(table_out[s], 32 * (FULL_NT // 2))
            flat = lambda a: a[:].rearrange("p i k -> p (i k)")
            link(dve.tensor_single_scalar(bits_i, src_i[:], 7, ALU.logical_shift_right))
            link(dve.tensor_copy(flat(src_tile), bits_i))
            link(dve.tensor_single_scalar(bits_i, src_i[:], P - 1, ALU.bitwise_and))
            link(dve.tensor_copy(flat(src_node), bits_i))

            dve.wait_ge(base_in, 32)
            link(dve.tensor_reduce(flag_f[:], flags_f[:], AX.X, ALU.max))
            dve.tensor_scalar(flag_i[:], flag_f[:], float(P - 1), None, ALU.is_gt).then_inc(flag_made, 1)

            for part in range(NPART):
                if part:
                    dve.wait_ge(totals_made, (2 * IPP + 1) * part)
                with dve.Fori(0, IPP) as i:
                    here = src_tile[:, bass.ds(i + part * IPP, 1), :].rearrange("p a (g c) -> p (a g) c", g=GROUPS)
                    for h in range(GROUPS):
                        ins = dve.tensor_tensor(
                            hits[:, bass.ds(i, 1), h].rearrange("p a t c -> p (a t) c"),
                            here[:, h:h + 1, :].to_broadcast([P, NT, GROUP]), tile_row[:], ALU.is_equal)
                    ins.then_inc(hits_made, 1)
                dve.wait_ge(hist_made, part + 1)
                link(dve.tensor_reduce(count[:], hist.rearrange("p (t c) -> p t c", c=GROUP), AX.X, ALU.add))
                link(dve.tensor_copy(count_i[:], count[:]))
                link(dve.tensor_single_scalar(count_i[:], count_i[:], 9, ALU.logical_shift_right))
                link(dve.tensor_scalar(blocks_f[:], count_i[:], 1.0, None, ALU.add))
                link(dve.tensor_tensor_scan(block_end[:, part, :], one_row[:], blocks_f[:], 0.0,
                                            ALU.mult, ALU.add))
                link(dve.tensor_tensor(base[:], block_end[:, part, :], blocks_f[:], ALU.subtract))
                dve.tensor_scalar(base[:], base[:], float(part * BPP), float(BLK * P), ALU.add, ALU.mult
                                  ).then_inc(base_made, 1)
                link(dve.tensor_scalar(tail_i[0:1, part * NT:(part + 1) * NT], block_end[0:1, part, :],
                                       float(part * BPP - 1), None, ALU.add))
                for h in range(2):
                    link(dve.tensor_scalar(cmp_tile[:], block_end[:, part, :], node_col[:, h:h + 1], None,
                                           ALU.is_le))
                    dve.tensor_reduce(tile_of[:, h:h + 1], cmp_tile[:], AX.X, ALU.add).then_inc(tileof_made, 1)
                    dve.wait_ge(tilerow_made, 2 * part + h + 1)
                    dve.tensor_copy(tile_f[0:1, part, h * P:(h + 1) * P], row_ps).then_inc(tilerow_kept, 1)
                with dve.Fori(0, IPP) as i:
                    i2 = dve.snap(i * 2 + 2 * part * IPP)
                    for h in range(GROUPS):
                        dve.wait_ge(ranks_made, i2 + (h + 1))
                        dve.wait_ge(rank_kept, i2 + (h - 1) if part or h else i * 2)
                        dve.tensor_tensor(masked[:, h].rearrange("p t c -> p (t c)"), ranks[h],
                                          hits[:, bass.ds(i, 1), h].rearrange("p a t c -> p (a t c)"),
                                          ALU.mult).then_inc(masked_made, 1)
                    for h in range(GROUPS):
                        dve.wait_ge(masked_made, i2 + (h + 1))
                        dve.tensor_reduce(place_f[:, bass.ds(i + part * IPP, 1), h * GROUP:(h + 1) * GROUP]
                                          .rearrange("p a c -> p (a c)"),
                                          masked[:, h].rearrange("p t c -> p c t"), AX.X, ALU.add
                                          ).then_inc(rank_kept, 1)
            dve.wait_ge(rank_kept, 2 * ITERS)
            for part in range(NPART):
                link(dve.tensor_copy(tile_i[0:1, part * BPP:(part + 1) * BPP], tile_f[0:1, part, 0:BPP]))
                link(dve.tensor_scalar(live_f[0:1, part * BPP:(part + 1) * BPP], tile_f[0:1, part, 0:BPP],
                                       float(NT), None, ALU.is_lt))
            dve.wait_ge(totals_made, (2 * IPP + 1) * NPART)
            link(dve.tensor_tensor(start_f, blk_iota[:], live_f, ALU.mult))
            dve.tensor_copy(start_i[:], start_f).then_inc(tables_made, 1)
            pad_f = src_i[:].bitcast(F32)
            link(dve.tensor_scalar(pad_f, flat(src_tile), float(NT), float(FAR), ALU.is_ge, ALU.mult))
            dve.tensor_tensor(flat(place), pad_f, flat(place_f), ALU.add).then_inc(place_made, 1)

            with dve.Fori(0, ITERS) as it:
                it1 = dve.snap(it + 1)
                for u in range(UNITS):
                    after(dve, spread_rows, u, it, it1)
                    slot_free(dve, kv_made, u, UNITS, it, it1)
                    dve.tensor_scalar(pick[:, u % 2], bank[u % 2][:], node_col[:, 0:1], None, ALU.is_equal
                                      ).then_inc(pick_made[u], 1)

            with dve.Fori(0, ITERS) as j:
                j1 = dve.snap(j + 1)
                j5 = dve.snap(j * BPI)
                j16 = dve.snap(j * 16 + 16)
                for s in range(BPI + 3):
                    if s < BPI:
                        k = s
                        dve.wait_ge(blk_in[k], j16)
                        slot_free(dve, turned_made, k, BPI, j, j1)
                        slot_free(dve, hotf_made, k, BPI, j, j1)
                        dve.tensor_tensor(hot[:, k % 2], node_row[:].unsqueeze(1).to_broadcast([P, BLK, P]),
                                          blk[:, k, :, TAG:TAG + 1].to_broadcast([P, BLK, P]),
                                          ALU.is_equal).then_inc(hot_made[k], 1)
                    if 1 <= s <= BPI:
                        k = s - 1
                        after(dve, q_made, k, j, j1)
                        slot_free(dve, score_made, k, BPI, j, j1)
                        dve.tensor_tensor(qk[:, k % 2], picked_q, blk[:, k, :, 0:D], ALU.mult
                                          ).then_inc(qk_made[k], 1)
                    if 2 <= s <= BPI + 1:
                        k = s - 2
                        after(dve, exp_made, k, j, j1)
                        dve.tensor_tensor(
                            msg[:, k % 2, :, 0:D].rearrange("p b (h f) -> p b h f", h=HEADS),
                            blk[:, k, :, D:2 * D].rearrange("p b (h f) -> p b h f", h=HEADS),
                            msg[:, k % 2, :, D:AW].unsqueeze(3).to_broadcast([P, BLK, HEADS, DH]),
                            ALU.mult).then_inc(msg_made[k], 1)
                    if 1 <= s <= BPI:
                        k = s - 1
                        after(dve, qk_made, k, j, j1)
                        slot_free(dve, clip_made, k, BPI, j, j1)
                        dve.tensor_reduce(score[:, k % 2].rearrange("p b h -> p (b h)"),
                                          qk[:, k % 2].rearrange("p b (h f) -> p (b h) f", h=HEADS),
                                          AX.X, ALU.add).then_inc(score_made[k], 1)
                    if s >= 3:
                        k = s - 3
                        tile = dve.value_load(tile_i[0:1, bass.ds(j5 + k, 1)], min_val=0, max_val=NT)
                        after(dve, sum_made, k, j, j1)
                        one_free(dve, acc_made, k, BPI, j, j1)
                        now = acc[:, bass.ds(tile, 1), :].rearrange("p a d -> p (a d)")
                        dve.tensor_tensor(now, now, sums, ALU.add).then_inc(acc_made[k], 1)
                    if 1 <= s <= BPI:
                        k = s - 1
                        after(dve, score_made, k, j, j1)
                        slot_free(dve, exp_made, k, BPI, j, j1)
                        dve.tensor_scalar(clipped[:, k % 2], score[:, k % 2], -CLIP, CLIP, ALU.max, ALU.min
                                          ).then_inc(clip_made[k], 1)

            f0 = [0]

            def chain(ins):
                f0[0] += 1
                ins.then_inc(fin, 1)
                dve.wait_ge(fin, f0[0])

            for k in range(BPI):
                dve.wait_ge(acc_made[k], ITERS)
            sum_v = acc[:, 0:NT, 0:D].rearrange("p t (h f) -> p t h f", h=HEADS)
            chain(dve.tensor_scalar(inv, acc[:, 0:NT, D:AW], EPS_W, None, ALU.add))
            chain(dve.reciprocal(inv, inv))
            chain(dve.tensor_tensor(y_all.rearrange("p t (h f) -> p t h f", h=HEADS), sum_v,
                                    inv.unsqueeze(3).to_broadcast([P, NT, HEADS, DH]), ALU.mult))
            dve.wait_ge(x_again, 32)
            full = [(slice(0, P), slice(0, FULL_NT)), (slice(0, NREST), slice(FULL_NT, NT))]
            for ps, ts in full:
                chain(dve.tensor_tensor(y_all[ps, ts], y_all[ps, ts], x_all[ps, ts], ALU.add))
                chain(dve.tensor_tensor(y_all[ps, ts], y_all[ps, ts], x_all[ps, ts], ALU.add))
            chain(dve.tensor_reduce(stat[:, 0, :], y_all, AX.X, ALU.add))
            chain(dve.tensor_scalar(stat[:, 0, :], stat[:, 0, :], 1.0 / D, None, ALU.mult))
            chain(dve.tensor_tensor(y_all, y_all, stat[:, 0, :].unsqueeze(2).to_broadcast([P, NT, D]),
                                    ALU.subtract))
            chain(dve.tensor_tensor(y2_all, y_all, y_all, ALU.mult))
            chain(dve.tensor_reduce(stat[:, 1, :], y2_all, AX.X, ALU.add))
            dve.tensor_scalar(stat[:, 2, :], stat[:, 1, :], 1.0 / D, EPS_LN, ALU.mult, ALU.add
                              ).then_inc(var_made, 1)
            dve.wait_ge(dev_made, 1)
            chain(dve.reciprocal(stat[:, 4, :], stat[:, 3, :]))
            dve.tensor_tensor(y_all, y_all, stat[:, 4, :].unsqueeze(2).to_broadcast([P, NT, D]), ALU.mult
                              ).then_inc(y_made, 1)


_INS = ["x", "src", "dst", "L0_gnn_qW", "L0_gnn_kW", "L0_gnn_vW"]


def kernel(**inputs):
    import numpy as np
    import concourse.bacc as bacc
    from concourse.bass_utils import run_bass_kernel_spmd

    nc = bacc.Bacc("TRN2", target_bir_lowering=False, num_devices=1)
    arrays, args = {}, []
    for name in _INS:
        a = np.ascontiguousarray(inputs[name])
        arrays[f"in_{name}"] = a
        args.append(nc.dram_tensor(f"in_{name}", a.shape, mybir.dt.from_np(a.dtype), kind="ExternalInput").ap())
    x, src, dst, wq, wk, wv = args
    out = nc.dram_tensor("out", arrays["in_x"].shape, F32, kind="ExternalOutput").ap()
    gnn_program(nc, x, src, dst, wq, wk, wv, out)
    r = run_bass_kernel_spmd(nc, [arrays], core_ids=[0])
    return r.results[0]["out"]
```

```python
from contextlib import ExitStack

import concourse.bass as bass
from concourse import mybir

ALU = mybir.AluOpType
ACT = mybir.ActivationFunctionType
AX = mybir.AxisListType
F32 = mybir.dt.float32
BF16 = mybir.dt.bfloat16
I32 = mybir.dt.int32
U32 = mybir.dt.uint32

P = 128
HEADS = 4
CLIP = 10.0
EPS_W = 1e-8
EPS_LN = 1e-5

ROWS_IT = 16
GROUP = 8
UNIT = 4
PARTS = (32, 34, 32)
BPI = 6
TURN = 7
TSLOT = 4
BLK = 4
WROW = 196
TAG = 192


def timetable(parts, gathers, tables):
    start = [sum(parts[:p]) for p in range(len(parts) + 1)]
    gstart = [sum(gathers[:p]) for p in range(len(parts) + 1)]
    pairs = start[-1] // 2
    early = max(parts[0] // 2, pairs - parts[0])
    before = [(None, None, i if i < early else None, i if i < tables else None)
              for i in range(max(early, tables))]
    rows, gather = [], 0
    for p, n in enumerate(parts):
        for i in range(n):
            this = gather if gather < gstart[p] else None
            rank = early + i if p == 0 and early + i < pairs else None
            rows.append((start[p] + i, this, rank, None))
            gather += this is not None
    rows += [(None, j, None, None) for j in range(gather, gstart[-1])]
    return before, rows


def segments(rows, alone, begins):
    runs = []
    for row in rows:
        last = runs[-1][-1] if runs else None
        if (last and not (alone(row) or alone(last) or begins(row))
                and all((a is None) == (b is None) and (a is None or b == a + 1) for a, b in zip(last, row))):
            runs[-1].append(row)
        else:
            runs.append([row])
    return [(r[0], len(r)) for r in runs]


def gnn_program(nc, x, src, dst, wq, wk, wv, out):
    N, D = x.shape
    E = src.shape[0]
    DH = D // HEADS
    NPART = len(PARTS)
    NT = -(-N // P)
    NB = NT + 1
    FULL_NT = N // P
    NREST = N - FULL_NT * P
    NTAB = (NT + 1) * P
    EIT = ROWS_IT * P
    ITERS = sum(PARTS)
    IT0 = [sum(PARTS[:p]) for p in range(NPART)]
    EFULL = E // EIT
    EREST = E - EFULL * EIT
    BROWS = BLK * P
    GITERS = [-(-(n * EIT // BROWS + NT) // BPI) for n in PARTS]
    J0 = [sum(GITERS[:p]) for p in range(NPART)]
    JS = sum(GITERS)
    NBLK = JS * BPI
    SORTED = NBLK * BROWS
    GROUPS = ROWS_IT // GROUP
    BATCHES = 2 * GROUPS
    UNITS = ROWS_IT // UNIT
    PAIRS = ROWS_IT // 2
    KVS = 3
    STEPS = max(BPI, UNITS + 1, BATCHES + 1)
    FAR = 1 << 20
    AW = D + HEADS
    assert ITERS == -(-E // EIT) <= P and all(n % 2 == 0 for n in PARTS)
    assert SORTED < FAR and FULL_NT % TSLOT == 0 and NT == FULL_NT + 1 and NT == TURN * TURN
    assert max(GITERS) * BPI <= 2 * P and GROUPS == 2 and UNITS == 4 and STEPS >= 5

    CHUNKS = [(NT * c // 4, NT * (c + 1) // 4) for c in range(4)]

    TI = FULL_NT // TSLOT
    before, rows = timetable(PARTS, GITERS, TI)

    kv3 = nc.dram_tensor("kv3_table", (NTAB, 3 * 2 * D), BF16).ap()
    rows_dram = nc.dram_tensor("sorted_rows", (SORTED, WROW), F32).ap()
    base_tmp = nc.dram_tensor("base_tmp", (ITERS, GROUPS), I32).ap()
    over_tmp = nc.dram_tensor("over_tmp", (ITERS, 1), F32).ap()

    with ExitStack() as ctx:
        def sb(name, shape, dt):
            return ctx.enter_context(nc.sbuf_tensor(name, shape, dt))

        def sem(name):
            return ctx.enter_context(nc.semaphore(name))

        def sems(name, n):
            return [sem(f"{name}{i}") for i in range(n)]

        ident_f = sb("ident_f", [P, P], F32)
        ident_b = sb("ident_b", [P, P], BF16)
        ones_b = sb("ones_b", [P, P], BF16)
        below_b = sb("below_b", [P, P], BF16)
        zeros_b = sb("zeros_b", [P, 3 * 2 * D], BF16)
        node_col = sb("node_col", [P, 2], F32)
        node_row = sb("node_row", [P, P, BLK], BF16)
        tile_row = sb("tile_row", [P, NB, GROUP], BF16)
        one_row = sb("one_row", [P, NT], F32)
        pad_rows = sb("pad_rows", [P, BLK, WROW], F32)
        weights = sb("weights", [D, 3 * D], F32)
        q3 = sb("q3", [P, NT + 1, 3, D], BF16)
        acc = sb("acc", [P, NT + 1, AW], F32)
        x_all = sb("x_all", [P, NT, D], F32)
        src_i = sb("src_i", [P, ITERS, ROWS_IT], I32)
        bits_i = sb("bits_i", [P, ITERS, ROWS_IT], I32)
        place = bits_i[:].bitcast(F32)
        src_tile = sb("src_tile", [P, ITERS, ROWS_IT], BF16)
        src_node = src_i[:].bitcast(F32)
        dst_col = sb("dst_col", [P, ITERS, ROWS_IT], I32)
        dst_local = sb("dst_local", [P, ROWS_IT, P], BF16)
        last3 = sb("last3", [P, 3, 3 * D], BF16)
        window = sb("window", [P, GROUPS, 3, 2 * D], BF16)
        dst_rows = sb("dst_rows", [P, 2, UNIT * P], BF16)
        pick = sb("pick", [P, 2, UNIT * P], BF16)
        payload = sb("payload", [P, ROWS_IT, WROW], F32)
        place_now = sb("place_now", [P, ROWS_IT], U32)
        dst_now = sb("dst_now", [P, GROUP], U32)
        far_rows = sb("far_rows", [P, GROUP, 3, 2 * D], BF16)
        hits = sb("hits", [P, BATCHES, NB, GROUP], BF16)
        masked = sb("masked", [P, 2, NB, GROUP], F32)
        carry = sb("carry", [P, BATCHES, NB], F32)
        count = sb("count", [P, NPART, NT], F32)
        count_i = sb("count_i", [P, NPART, NT], I32)
        blocks_f = sb("blocks_f", [P, NPART, NT], F32)
        block_end = sb("block_end", [P, NPART, NT], F32)
        base = sb("base", [P, NPART, NB], F32)
        cmp_tile = sb("cmp_tile", [P, 2, NT], F32)
        tile_of = sb("tile_of", [P, 2 * NPART], F32)
        tail_i = sb("tail_i", [1, NPART * NT], I32)
        tile_i = sb("tile_i", [1, NBLK], I32)
        start_i = sb("start_i", [1, NBLK], I32)
        span = sb("span", [P, 2, GROUPS], F32)
        over_f = sb("over_f", [P, 1], F32)
        span_i = sb("span_i", [P, GROUPS], I32)
        base_i = sb("base_i", [1, ITERS * GROUPS], I32)
        overs_f = sb("overs_f", [1, ITERS], F32)
        flag_f = sb("flag_f", [1, 1], F32)
        flag_i = sb("flag_i", [1, 1], I32)
        WORK = 15800
        work = sb("work", [P, WORK], F32)

        def share(at, shape, dt):
            n = 1
            for d in shape:
                n *= d
            words = n // 2 if dt == BF16 else n
            assert at + words <= WORK
            v = work[:, at:at + words]
            v = v if dt == F32 else v.bitcast(dt)
            if len(shape) == 1:
                return v, at + words
            names = " ".join(f"d{i}" for i in range(len(shape)))
            return v.rearrange(f"p ({names}) -> p {names}",
                               **{f"d{i}": d for i, d in enumerate(shape)}), at + words

        edge_i, at = share(0, [EIT], I32)
        edge_f, at = share(at, [EIT], F32)
        dest_i, at = share(at, [EIT], I32)
        dest_f, at = share(at, [EIT], F32)
        x_in, at = share(at, [TSLOT, D], F32)
        xT, at = share(at, [TSLOT, P], F32)
        parts3, at = share(at, [TSLOT, 3, 3 * D], BF16)
        rest, at = share(at, [TSLOT, 3 * D], F32)
        blk_iota, at = share(0, [NBLK], F32)
        tile_f, at = share(at, [NBLK], F32)
        live_f, at = share(at, [NBLK], F32)
        start_f, at = share(at, [NBLK], F32)
        blk, at = share(0, [BPI, BLK, WROW], F32)
        tags, at = share(at, [BPI, BLK], BF16)
        hot, at = share(at, [BPI, P, BLK], BF16)
        hot_f, at = share(at, [BPI, BLK, P], F32)
        hot_T, at = share(at, [BPI, BLK, P], BF16)
        qk, at = share(at, [BPI, BLK, D], F32)
        score, at = share(at, [BPI, BLK * HEADS], F32)
        clipped, at = share(at, [BPI, BLK, HEADS], F32)
        msg, at = share(at, [BPI, BLK, AW], F32)
        sq_all, at = share(0, [NT, D], F32)
        inv, at = share(at, [NT, HEADS], F32)
        stat, at = share(at, [5, NT], F32)

        def ps(name, shape):
            return ctx.enter_context(nc.psum_tensor(name, shape, F32))

        rows_bank = ps("rows_bank", [P, 512])
        kv_bank = [ps(f"kv_bank{i}", [P, 512]) for i in range(KVS)]
        q_bank = ps("q_bank", [P, 512])
        turn_bank = ps("turn_bank", [P, 512])
        sum_bank = ps("sum_bank", [P, 512])
        rank_bank = ps("rank_bank", [P, 512])
        turned = turn_bank[:, 0:BLK * P // 2].bitcast(BF16).rearrange("p (b n) -> p b n", b=BLK)
        sums = sum_bank[:, 0:AW]
        picked_q = q_bank[:, 0:BLK * D].rearrange("p (b d) -> p b d", b=BLK)
        ranks = [b[:, 0:NB * GROUP] for b in (rank_bank, q_bank)]
        totals = sum_bank[:, 0:NB]
        hist = q_bank[:, 0:NB * GROUP]
        xT_ps = rows_bank[0:D, 0:TSLOT * P].rearrange("p (s n) -> p s n", s=TSLOT)
        proj_ps = [b[:, 0:3 * D] for b in (*kv_bank, turn_bank)]
        turn_ps = [b[:, 0:P] for b in (rows_bank, rank_bank)]
        tile_ps = [b[0:1, h * 2 * P:(h + 1) * 2 * P] for b in (rows_bank, rank_bank) for h in range(2)]

        consts = sem("consts")
        loads = sem("loads")
        edge_pads = sem("edge_pads")
        edges_in = sem("edges_in")
        edges_f = sem("edges_f")
        turned_edges = sem("turned_edges")
        kept_edges = sem("kept_edges")
        dve_step = sem("dve_step")
        span_made = sem("span_made")
        span_out = sem("span_out")
        base_in = sem("base_in")
        local_made = sem("local_made")
        flag_made = sem("flag_made")
        x_loaded = sem("x_loaded")
        xT_made = sem("xT_made")
        xT_kept = sem("xT_kept")
        proj_made = sem("proj_made")
        high_made = sem("high_made")
        split_step = sem("split_step")
        low_made = sem("low_made")
        q_kept = sem("q_kept")
        table_out = sem("table_out")
        rest_out = sem("rest_out")
        hits_made = sem("hits_made")
        count_used = sem("count_used")
        hist_made = sem("hist_made")
        count_made = sem("count_made")
        tiles_made = sem("tiles_made")
        tilerow_made = sem("tilerow_made")
        tables_made = sem("tables_made")
        totals_made = sem("totals_made")
        carry_made = sem("carry_made")
        ranks_made = sem("ranks_made")
        masked_made = sem("masked_made")
        place_made = sem("place_made")
        tails_out = sems("tails_out", NPART)
        window_in = sems("window_in", GROUPS)
        spread_rows = sems("spread_rows", UNITS)
        rows_kept = sems("rows_kept", UNITS)
        pick_made = sems("pick_made", UNITS)
        kv_made = sems("kv_made", PAIRS)
        payload_made = sems("payload_made", PAIRS)
        tags_made = sems("tags_made", GROUPS)
        scattered = sems("scattered", UNITS)
        slow_step = sem("slow_step")
        fetched = sem("fetched")
        pool_turn = sem("pool_turn")
        blk_in = sems("blk_in", BPI)
        tag_made = sems("tag_made", BPI)
        hot_made = sems("hot_made", BPI)
        turned_made = sems("turned_made", BPI)
        hotT_made = sems("hotT_made", BPI)
        q_made = sems("q_made", BPI)
        qk_made = sems("qk_made", BPI)
        score_made = sem("score_made")
        clip_made = sems("clip_made", BPI)
        exp_made = sems("exp_made", BPI)
        msg_made = sems("msg_made", BPI)
        sum_made = sems("sum_made", BPI)
        acc_made = sems("acc_made", BPI)
        square_made = sem("square_made")
        centered = sem("centered")
        y_made = sem("y_made")
        stored = sem("stored")

        NCONST = 20

        def lagged(s, lag, j, j1, drain=False):
            if s >= lag:
                return None if drain or s - lag >= BPI else (s - lag, j1)
            return None if isinstance(j, int) and j == 0 else (s - lag + BPI, j)

        def one_free(eng, sem_list, k, j, j1):
            if k:
                eng.wait_ge(sem_list[k - 1], j1)
            elif not (isinstance(j, int) and j == 0):
                eng.wait_ge(sem_list[-1], j)

        def slot_free(eng, sem_list, n, slots, it, it1):
            if n >= slots:
                eng.wait_ge(sem_list[n - slots], it1)
            elif not (isinstance(it, int) and it == 0):
                eng.wait_ge(sem_list[max(m for m in range(len(sem_list)) if m % slots == n)], it)

        def plus(eng, v, by):
            return v + by if isinstance(v, int) else eng.snap(v + by)

        def times(eng, v, by, more=0):
            return v * by + more if isinstance(v, int) else eng.snap(v * by + more)

        def loop(eng, n, emit):
            emit(0)
            with eng.Fori(0, n - 1) as i:
                emit(eng.snap(i + 1))

        COUNTED = ITERS * GROUPS

        def alone(row):
            return 0 in row

        def begins(row):
            return row[0] in IT0 or row[1] in J0 or (row[2] is not None and 2 * row[2] in IT0)

        def run(eng, rows, emit, enter=None, begins=begins):
            for first, n in segments(rows, alone, begins):
                if enter:
                    enter(*first)
                if n == 1:
                    emit(*first)
                else:
                    with eng.Fori(0, n) as i:
                        emit(*(None if v is None else eng.snap(i + v) for v in first))

        def words(eng, regs, table, at, top):
            eng.reg_load(regs, table[0:1, bass.ds(at, len(regs))])
            return [eng.snap(x, min_val=0, max_val=top) for x in regs]

        block = ctx.enter_context(nc.Block())

        @block.gpsimd
        def _(pool):
            pool.memset(ident_f[:], 0.0).then_inc(consts, 1)
            pool.memset(ident_b[:], 0.0).then_inc(consts, 1)
            pool.memset(below_b[:], 1.0).then_inc(consts, 1)
            pool.wait_ge(consts, 3)
            for m in (ident_f, ident_b):
                pool.affine_select(out=m[:], in_=m[:], compare_op=ALU.not_equal, fill=1.0, base=0,
                                   pattern=[[-1, P]], channel_multiplier=1).then_inc(consts, 1)
            pool.affine_select(out=below_b[:], in_=below_b[:], compare_op=ALU.is_gt, fill=0.0, base=0,
                               pattern=[[1, P]], channel_multiplier=-1).then_inc(consts, 1)
            pool.memset(last3[:], 0.0).then_inc(consts, 1)
            pool.memset(q3[:, FULL_NT:NT + 1], 0.0).then_inc(consts, 1)
            for held, pattern, by in ((node_col, [[P, 2]], 1), (node_row, [[1, P], [0, BLK]], 0),
                                      (tile_row, [[1, NB], [0, GROUP]], 0)):
                pool.iota(held[:], pattern, base=0, channel_multiplier=by,
                          allow_small_or_imprecise_dtypes=True).then_inc(consts, 1)
            pool.memset(pad_rows[:], 0.0).then_inc(consts, 1)
            pool.wait_ge(consts, 12)
            pool.memset(pad_rows[:, :, TAG:TAG + 1], -1.0).then_inc(consts, 1)
            pool.memset(ones_b[:], 1.0).then_inc(consts, 1)
            pool.memset(zeros_b[:], 0.0).then_inc(consts, 1)
            pool.memset(one_row[:], 1.0).then_inc(consts, 1)
            pool.memset(acc[:], 0.0).then_inc(consts, 1)
            pool.memset(payload[:, :, TAG:WROW], 0.0).then_inc(consts, 1)
            pool.memset(x_all[:, FULL_NT, :], 0.0).then_inc(consts, 1)
            pool.memset(base[:, :, NT:NB], float(FAR)).then_inc(consts, 1)
            pool.wait_ge(kept_edges, 2 * ROWS_IT)
            pool.iota(blk_iota[0:1, :], [[1, NBLK]], base=0, channel_multiplier=0,
                      allow_small_or_imprecise_dtypes=True).then_inc(consts, 1)

            pool.wait_ge(flag_made, 1)
            over = pool.value_load(flag_i[0:1, 0:1], min_val=0, max_val=1)
            pool.wait_ge(table_out, 16 * FULL_NT)
            pool.wait_ge(rest_out, 32)
            last_place = pool.to_reg(SORTED - 1)
            last_row = pool.to_reg(NTAB - 1)

            def scatter(u, it1):
                pool.wait_ge(payload_made[2 * u + 1], it1)
                pool.sem_inc(pool_turn, 1)
                for k in range(UNIT * u, UNIT * (u + 1)):
                    pool.indirect_dma_start(
                        out=rows_dram, out_offset=bass.IndirectOffsetOnAxis(ap=place_now[:, k:k + 1], axis=0),
                        in_=payload[:, k, :], in_offset=None,
                        bounds_check=last_place, oob_is_err=False).then_inc(scattered[u], 16)

            def fast(it):
                it1 = pool.snap(it + 1)
                it2 = pool.snap(it * 2 + 2)
                for u in range(UNITS):
                    if u % 2 == 0:
                        pool.wait_ge(tags_made[u // 2], it2)
                    scatter(u, it1)

            COUNTS = 3

            def slow(it):
                it1 = pool.snap(it + 1)
                it2 = pool.snap(it * 2 + 2)
                for g in range(GROUPS):
                    copied, added, summed = (
                        pool.snap(it * (GROUPS * COUNTS) + (g * COUNTS + n)) for n in (1, 2, 3))
                    gathered = pool.snap(it * (GROUPS * GROUP * 16) + (g + 1) * GROUP * 16)
                    for u in range(2 * g, 2 * g + 2):
                        pool.wait_ge(payload_made[2 * u + 1], it1)
                    pool.wait_ge(tags_made[g], it2)
                    pool.tensor_copy(dst_now[:], dst_col[:, bass.ds(it, 1), g * GROUP:(g + 1) * GROUP]
                                     .rearrange("p a b -> p (a b)")).then_inc(slow_step, 1)
                    pool.wait_ge(slow_step, copied)
                    pool.sem_inc(pool_turn, 1)
                    for k in range(GROUP):
                        pool.indirect_dma_start(
                            out=far_rows[:, k].rearrange("p a b -> p (a b)"), out_offset=None,
                            in_=kv3, in_offset=bass.IndirectOffsetOnAxis(ap=dst_now[:, k:k + 1], axis=0),
                            bounds_check=last_row, oob_is_err=False).then_inc(fetched, 16)
                    to = payload[:, g * GROUP:(g + 1) * GROUP, 0:2 * D]
                    pool.wait_ge(fetched, gathered)
                    pool.tensor_tensor(to, far_rows[:, :, 0, :], far_rows[:, :, 1, :], ALU.add
                                       ).then_inc(slow_step, 1)
                    pool.wait_ge(slow_step, added)
                    pool.tensor_tensor(to, to, far_rows[:, :, 2, :], ALU.add).then_inc(slow_step, 1)
                    pool.wait_ge(slow_step, summed)
                    for u in range(2 * g, 2 * g + 2):
                        scatter(u, it1)

            def spread(one):
                for p in range(NPART):
                    pool.wait_ge(tails_out[p], 16 * NT)
                    with pool.Fori(IT0[p], IT0[p] + PARTS[p]) as it:
                        one(it)

            with pool.If(over == 0):
                spread(fast)
            with pool.Else():
                spread(slow)

        @block.sync
        def _(sp):
            sp.wait_ge(edge_pads, 2)
            for flat, held in ((src, edge_i), (dst, dest_i)):
                sp.dma_start(held[0:EFULL, :], flat[0:EFULL * EIT].rearrange("(i e) -> i e", e=EIT)
                             ).then_inc(edges_in, 16)
                sp.dma_start(held[EFULL:EFULL + 1, 0:EREST],
                             flat[EFULL * EIT:E].rearrange("(i e) -> i e", i=1)).then_inc(edges_in, 16)
            for n, w in enumerate((wk, wv, wq)):
                sp.dma_start(weights[:, n * D:(n + 1) * D], w).then_inc(loads, 16)

            tail_regs = [sp.alloc_register(f"tail{k}") for k in range(TURN)]
            lo_regs = [sp.alloc_register(f"window{g}") for g in range(GROUPS)]
            start_regs = [sp.alloc_register(f"start{k}") for k in range(BPI)]
            rows_of_block = rows_dram.rearrange("(b p k) w -> b p k w", p=P, k=BLK)

            def of_block(b):
                return rows_of_block[bass.ds(b, 1)].rearrange("b p k w -> (b p) k w")

            def table_rows(at, parts, done):
                sp.dma_start(kv3[at, :].rearrange("p (a b) -> p a b", a=3), parts[:, :, 0:2 * D]
                             ).then_inc(done, 16)

            def outs(j):
                for s in range(TSLOT):
                    sp.wait_ge(low_made, times(sp, j, TSLOT, s + 1))
                    table_rows(bass.ds(j * (TSLOT * P) + s * P, P), parts3[:, s], table_out)

            def features(j):
                for s in range(TSLOT):
                    if not isinstance(j, int):
                        sp.wait_ge(xT_made, j)
                    sp.dma_start(x_in[:, s, :], x[bass.ds(j * (TSLOT * P) + s * P, P), :]
                                 ).then_inc(x_loaded, 16)
                if not isinstance(j, int):
                    outs(sp.snap(j - 1))

            def pad_tails(at, regs, p):
                for b in words(sp, regs, tail_i, at, NBLK - 1):
                    sp.dma_start(of_block(b), pad_rows[:]).then_inc(tails_out[p], 16)

            def features_and_tails(j):
                features(j)
                if isinstance(j, int):
                    sp.wait_ge(consts, NCONST)
                    sp.wait_ge(tables_made, 1)
                pad_tails(times(sp, j, TSLOT), tail_regs[0:TSLOT], 0)

            loop(sp, TI, features_and_tails)
            pad_tails(FULL_NT, tail_regs[0:1], 0)
            sp.wait_ge(xT_made, TI)
            sp.dma_start(x_in[0:NREST, 0, :], x[FULL_NT * P:N, :]).then_inc(x_loaded, 16)
            outs(TI - 1)
            sp.wait_ge(low_made, FULL_NT + 1)
            table_rows(slice(FULL_NT * P, NT * P), last3, rest_out)
            sp.wait_ge(consts, NCONST)
            sp.dma_start(kv3[NT * P:NTAB, :], zeros_b[:]).then_inc(rest_out, 16)
            sp.dma_start(x_all[:, 0:FULL_NT, :], x[0:FULL_NT * P, :].rearrange("(t p) d -> p t d", p=P)
                         ).then_inc(loads, 16)
            sp.dma_start(x_all[0:NREST, FULL_NT, :], x[FULL_NT * P:N, :]).then_inc(loads, 16)

            def with_tails(row):
                it, j, *_ = row
                if it is None:
                    return it, j, None
                p = max(q for q in range(NPART) if IT0[q] <= it)
                n = it - IT0[p]
                return it, j, (p + 1) * TURN + n if p + 1 < NPART and n < TURN else None

            sp.wait_ge(table_out, 16 * FULL_NT)
            sp.wait_ge(rest_out, 32)
            sp.wait_ge(base_in, 32)
            part = [0]

            def enter(it, j, n):
                if n is not None:
                    part[0] = n // TURN
                if j in J0:
                    p = J0.index(j)
                    for u in range(UNITS):
                        sp.wait_ge(scattered[u], 16 * UNIT * (IT0[p] + PARTS[p]))

            def emit(it, j, n):
                def window_of(g, lo):
                    if not (isinstance(it, int) and it == 0):
                        sp.wait_ge(kv_made[4 * g + 3], it)
                    sp.dma_start(window[:, g].rearrange("p a b -> p (a b)"), kv3[bass.ds(lo, P), :]
                                 ).then_inc(window_in[g], 16)

                def load(k, b):
                    if not (isinstance(j, int) and j == 0):
                        sp.wait_ge(msg_made[k], j)
                    sp.dma_start(blk[:, k], of_block(b)).then_inc(blk_in[k], 16)

                if it is not None:
                    los = words(sp, lo_regs, base_i, it * GROUPS, N - 1)
                    window_of(0, los[0])
                if j is not None:
                    starts = words(sp, start_regs, start_i, j * BPI, NBLK - 1)
                    for k in range(2):
                        load(k, starts[k])
                if it is not None:
                    window_of(1, los[1])
                if j is not None:
                    for k in range(2, BPI):
                        load(k, starts[k])
                if n is not None:
                    pad_tails(times(sp, n, TURN), tail_regs, part[0])

            sp_rows = [with_tails(row) for row in rows]
            run(sp, sp_rows, emit, enter,
                begins=lambda row: row[0] in IT0 or row[1] in J0 or (row[2] is not None and row[2] % TURN == 0))

            for c, (lo, hi) in enumerate(CHUNKS):
                sp.wait_ge(y_made, c + 1)
                full = min(hi, FULL_NT)
                sp.dma_start(out[lo * P:full * P, :].rearrange("(t p) d -> p t d", p=P),
                             acc[:, lo:full, 0:D]).then_inc(stored, 16)
                if hi == NT:
                    sp.dma_start(out[FULL_NT * P:N, :], acc[0:NREST, FULL_NT, 0:D]).then_inc(stored, 16)
            sp.wait_ge(stored, 16 * (len(CHUNKS) + 1))

        @block.scalar
        def _(act):
            act.wait_ge(span_made, 1)
            act.dma_start(base_tmp, span_i[0:ITERS, :]).then_inc(span_out, 16)
            act.dma_start(over_tmp, over_f[0:ITERS, :]).then_inc(span_out, 16)
            act.wait_ge(span_out, 32)
            act.dma_start(base_i[:], base_tmp.rearrange("(o a) b -> o (a b)", o=1)).then_inc(base_in, 16)
            act.dma_start(overs_f[:], over_tmp.rearrange("(o a) b -> o (a b)", o=1)).then_inc(base_in, 16)
            act.wait_ge(consts, NCONST)

            def high(s, j, n, parts):
                act.wait_ge(proj_made, times(act, j, TSLOT, s + 1))
                act.activation(parts[0:n, 0, :], proj_ps[s][0:n, :], ACT.Copy).then_inc(high_made, 1)

            def keep_q(s, j, n, parts, to):
                act.wait_ge(low_made, times(act, j, TSLOT, s + 1))
                act.activation(to, parts[0:n, :, 2 * D:3 * D], ACT.Copy).then_inc(q_kept, 1)

            def enter(it, j, r, t):
                if it == 0:
                    act.wait_ge(xT_made, TI + 1)
                    act.activation(xT[0:D, 0, 0:NREST], xT_ps[:, 0, 0:NREST], ACT.Copy).then_inc(xT_kept, 1)
                    high(0, TI, NREST, last3)
                    keep_q(0, TI, NREST, last3, q3[0:NREST, FULL_NT])
                if it in IT0:
                    p = IT0.index(it)
                    act.wait_ge(place_made, 2 * (IT0[p] + PARTS[p]))

            def emit(it, j, r, t, drain=False):
                if it is not None:
                    it1, it64 = plus(act, it, 1), times(act, it, 16 * UNIT)
                    here = bass.ds(it, 1)
                if j is not None:
                    j1, j16 = plus(act, j, 1), times(act, j, 16, 16)

                for s in range(STEPS):
                    if t is not None:
                        if s == 1:
                            act.wait_ge(xT_made, plus(act, t, 1))
                            act.activation(xT[0:D], xT_ps, ACT.Copy).then_inc(xT_kept, 1)
                        if s == 2:
                            if not isinstance(t, int):
                                act.wait_ge(table_out, times(act, t, 16 * TSLOT))
                            for q in range(TSLOT):
                                high(q, t, P, parts3[:, q])
                        if s == 4:
                            for q in range(TSLOT):
                                keep_q(q, t, P, parts3[:, q],
                                       q3[:, bass.ds(times(act, t, TSLOT, q), 1), :, :].rearrange("p o a d -> p (o a) d"))
                    if it is not None and s < UNITS:
                        act.wait_ge(spread_rows[s], it1)
                        slot_free(act, pick_made, s, 2, it, it1)
                        act.activation(dst_rows[:, s % 2], rows_bank[:], ACT.Copy).then_inc(rows_kept[s], 1)
                    if j is not None:
                        if at := lagged(s, 3, j, j1, drain):
                            k, n = at
                            act.wait_ge(clip_made[k], n)
                            act.activation(msg[:, k, :, D:AW], clipped[:, k], ACT.Exp).then_inc(exp_made[k], 1)
                        if at := lagged(s, 0, j, j1, drain):
                            k, n = at
                            act.wait_ge(blk_in[k], j16)
                            act.activation(tags[:, k, :].unsqueeze(2), blk[:, k, :, TAG:TAG + 1], ACT.Copy
                                           ).then_inc(tag_made[k], 1)
                    if it is not None and s in (0, 2):
                        g = s // 2
                        cols = slice(g * GROUP, (g + 1) * GROUP)
                        if not (isinstance(it, int) and it == 0):
                            act.wait_ge(scattered[2 * g], it64)
                            act.wait_ge(scattered[2 * g + 1], it64)
                        act.activation(place_now[:, cols], place[:, here, cols].rearrange("p a b -> p (a b)"),
                                       ACT.Copy).then_inc(tags_made[g], 1)
                        act.activation(payload[:, cols, TAG:TAG + 1].rearrange("p a b -> p (a b)"),
                                       src_node[:, here, cols].rearrange("p a b -> p (a b)"), ACT.Copy
                                       ).then_inc(tags_made[g], 1)
                    if j is not None:
                        if at := lagged(s, 1, j, j1, drain):
                            k, n = at
                            act.wait_ge(turned_made[k], n)
                            act.activation(hot_T[:, k], turned, ACT.Copy).then_inc(hotT_made[k], 1)
                            act.wait_ge(hot_made[k], n)
                            act.activation(hot_f[:, k], hot[:, k].rearrange("p n b -> p b n"), ACT.Copy)
                    if it is not None and 1 <= s <= UNITS:
                        for n in (2 * s - 2, 2 * s - 1):
                            act.wait_ge(kv_made[n], it1)
                            act.activation(payload[:, 2 * n:2 * n + 2, 0:2 * D],
                                           kv_bank[n % KVS][:, 0:4 * D].rearrange("p (b d) -> p b d", b=2),
                                           ACT.Copy).then_inc(payload_made[n], 1)

            run(act, before + rows, emit, enter)
            emit(None, JS, None, None, drain=True)

            for c, (lo, hi) in enumerate(CHUNKS):
                act.wait_ge(centered, c + 1)
                act.activation(sq_all[:, lo:hi, :], acc[:, lo:hi, 0:D], ACT.Square).then_inc(square_made, 1)
            act.wait_ge(centered, len(CHUNKS) + 1)
            act.activation(stat[:, 3, :], stat[:, 2, :], ACT.Sqrt).then_inc(square_made, 1)

        @block.tensor
        def _(pe):
            pe.wait_ge(consts, NCONST)
            pe.wait_ge(edges_f, 2)
            for n in range(2 * ROWS_IT):
                held, k = (edge_f, dest_f)[n // ROWS_IT], n % ROWS_IT
                if n >= 2:
                    pe.wait_ge(kept_edges, n - 1)
                pe.transpose(turn_ps[n % 2][:, 0:ITERS], held[0:ITERS, k * P:(k + 1) * P],
                             ident_f[0:ITERS, 0:ITERS]).then_inc(turned_edges, 1)
            pe.wait_ge(kept_edges, 2 * ROWS_IT)

            pairs = [0]
            for p in range(NPART):
                if p:
                    pe.wait_ge(count_made, p)
                pe.matmul(hist, ones_b[:], zeros_b[:, 0:NB * GROUP], start=True, stop=False)
                with pe.Fori(0, PARTS[p] // 2) as i:
                    for q in range(4):
                        pe.wait_ge(hits_made, pe.snap(i * 4 + (4 * pairs[0] + q + 1)))
                        pe.matmul(hist, ones_b[:], hits[:, q].rearrange("p t c -> p (t c)"),
                                  start=False, stop=False).then_inc(count_used, 1)
                pairs[0] += PARTS[p] // 2
                pe.matmul(hist, ones_b[:], zeros_b[:, 0:NB * GROUP], start=False, stop=True
                          ).then_inc(hist_made, 1)

            pe.wait_ge(tiles_made, 1)
            for c in range(2 * NPART):
                mm = pe.matmul(tile_ps[c // 2][:, (c % 2) * P:(c % 2 + 1) * P], tile_of[:, c:c + 1], ident_f[:],
                               start=True, stop=True)
            mm.then_inc(tilerow_made, 1)
            pe.wait_ge(tables_made, 1)

            pe.wait_ge(loads, 48)

            def turn(s, n, last):
                mm = pe.transpose(xT_ps[:, s, 0:n], x_in[0:n, s, :], ident_f[0:n, 0:n])
                if last:
                    mm.then_inc(xT_made, 1)

            def project(s, j, n):
                if not (isinstance(j, int) and j == 0):
                    pe.wait_ge(split_step, times(pe, j, 2 * TSLOT, s + 1 - 2 * TSLOT))
                pe.matmul(proj_ps[s][0:n, :], xT[0:D, s, 0:n], weights[:], start=True, stop=True
                          ).then_inc(proj_made, 1)

            pe.wait_ge(local_made, GROUPS)
            tile_regs = [pe.alloc_register(f"tile{k}") for k in range(BPI)]

            part = [0]

            def enter(it, j, r, t):
                if r is not None and 2 * r in IT0:
                    part[0] = IT0.index(2 * r)
                if it == 0:
                    pe.wait_ge(xT_kept, TI)
                    pe.wait_ge(x_loaded, 16 * (FULL_NT + 1))
                    turn(0, NREST, True)
                    pe.wait_ge(xT_kept, TI + 1)
                    project(0, TI, NREST)
                    pe.wait_ge(split_step, 2 * FULL_NT + 2)
                    pe.wait_ge(q_kept, FULL_NT + 1)
                if j == 0:
                    pe.wait_ge(masked_made, ITERS * GROUPS)
                    pe.wait_ge(carry_made, ITERS * GROUPS + NPART)

            def emit(it, j, r, t, drain=False):
                if it is not None:
                    it1, it16 = plus(pe, it, 1), times(pe, it, 16, 16)
                    sel = ident_b[0:ITERS, bass.ds(it, 1)].to_broadcast([ITERS, P])
                if j is not None:
                    j1 = plus(pe, j, 1)
                    LQ = 2
                    if drain:
                        tiles = words(pe, tile_regs[0:LQ], tile_i, j * BPI - LQ, NT)
                    elif isinstance(j, int) and j == 0:
                        tiles = [None] * LQ + words(pe, tile_regs[LQ:BPI], tile_i, 0, NT)
                    else:
                        tiles = words(pe, tile_regs, tile_i, j * BPI - LQ, NT)
                def total(h):
                    pe.wait_ge(hits_made, times(pe, r, BATCHES, COUNTED + h + 1))
                    pe.wait_ge(carry_made, times(pe, r, BATCHES, h + part[0] + 1))
                    for c in range(GROUP):
                        mm = pe.matmul(totals, ones_b[:], hits[:, h, :, c:c + 1].rearrange("p t c -> p (t c)"),
                                       start=(c == 0), stop=(c == GROUP - 1))
                    mm.then_inc(totals_made, 1)

                def rank(h):
                    now = hits[:, h]
                    to = ranks[h % 2].rearrange("p (t c) -> p t c", c=GROUP)
                    if h >= 2 or not isinstance(r, int) or r:
                        pe.wait_ge(masked_made, times(pe, r, BATCHES, h - 1))
                    pe.matmul(to, below_b[:], now, start=True, stop=False)
                    for c in range(GROUP - 1):
                        pe.matmul(to[:, :, c + 1:], ones_b[:],
                                  now[:, :, c:c + 1].to_broadcast([P, NB, GROUP - 1 - c]),
                                  start=False, stop=False)
                    pe.matmul(to, ident_f[:], carry[:, h].unsqueeze(2).to_broadcast([P, NB, GROUP]),
                              start=False, stop=True).then_inc(ranks_made, 1)

                for s in range(STEPS):
                    if t is not None and s == 0:
                        if not isinstance(t, int):
                            pe.wait_ge(xT_kept, t)
                        pe.wait_ge(x_loaded, times(pe, t, 16 * TSLOT, 16 * TSLOT))
                        for q in range(TSLOT):
                            turn(q, P, q == TSLOT - 1)
                    if t is not None and s == 1:
                        pe.wait_ge(xT_kept, plus(pe, t, 1))
                        for q in range(TSLOT):
                            project(q, t, P)
                    if it is not None and s < UNITS:
                        u = s
                        slot_free(pe, rows_kept, u, 1, it, it1)
                        pe.matmul(rows_bank[:], sel,
                                  dst_local[0:ITERS, UNIT * u:UNIT * (u + 1), :].rearrange("p a b -> p (a b)"),
                                  start=True, stop=True).then_inc(spread_rows[u], 1)
                    if j is not None:
                        if at := lagged(s, 2, j, j1, drain):
                            k, n = at
                            pe.wait_ge(hotT_made[k], n)
                            one_free(pe, qk_made, k, j, n)
                            for b in range(BLK):
                                for a in range(3):
                                    mm = pe.matmul(picked_q[:, b, :], hot_T[:, k, b, :],
                                                   q3[:, bass.ds(tiles[s], 1), a, :].rearrange("p a d -> p (a d)"),
                                                   start=(a == 0), stop=(a == 2))
                            mm.then_inc(q_made[k], 1)
                        if at := lagged(s, 1, j, j1, drain):
                            k, n = at
                            pe.wait_ge(hot_made[k], n)
                            one_free(pe, hotT_made, k, j, n)
                            for b in range(BLK):
                                mm = pe.transpose(turned[:, b, :], hot[:, k, :, b], ident_b[:])
                            mm.then_inc(turned_made[k], 1)
                    if it is not None and 1 <= s <= UNITS:
                        u = s - 1
                        pe.wait_ge(pick_made[u], it1)
                        if u % 2 == 0:
                            pe.wait_ge(window_in[u // 2], it16)
                        for n in (2 * u, 2 * u + 1):
                            slot_free(pe, payload_made, n, KVS, it, it1)
                            for k in range(2):
                                to = kv_bank[n % KVS][:, k * 2 * D:(k + 1) * 2 * D]
                                row = (n % 2) * 2 + k
                                for a in range(3):
                                    mm = pe.matmul(to, pick[:, u % 2, row * P:(row + 1) * P],
                                                   window[:, u // 2, a, :], start=(a == 0), stop=(a == 2))
                            mm.then_inc(kv_made[n], 1)
                    if r is not None and 1 <= s <= BATCHES:
                        total(s - 1)
                        rank(s - 1)
                    if j is not None:
                        if at := lagged(s, 3, j, j1, drain):
                            k, n = at
                            pe.wait_ge(msg_made[k], n)
                            one_free(pe, acc_made, k, j, n)
                            for b in range(BLK):
                                mm = pe.matmul(sums, hot_f[:, k, b, :], msg[:, k, b, :],
                                               start=(b == 0), stop=(b == BLK - 1))
                            mm.then_inc(sum_made[k], 1)

            run(pe, before + rows, emit, enter)
            emit(None, JS, None, None, drain=True)

        @block.vector
        def _(dve):
            step = [0]

            def link(ins):
                step[0] += 1
                ins.then_inc(dve_step, 1)
                dve.wait_ge(dve_step, step[0])

            dve.memset(edge_i, NT * P).then_inc(edge_pads, 1)
            dve.memset(dest_i, N - 1).then_inc(edge_pads, 1)
            dve.wait_ge(edges_in, 64)
            dve.tensor_copy(edge_f[0:ITERS], edge_i[0:ITERS]).then_inc(edges_f, 1)
            dve.tensor_copy(dest_f[0:ITERS], dest_i[0:ITERS]).then_inc(edges_f, 1)
            dve.wait_ge(edges_f, 2)
            grouped = dest_f[0:ITERS].rearrange("p (g e) -> p g e", g=GROUPS)
            link(dve.tensor_reduce(span[0:ITERS, 0, :], grouped, AX.X, ALU.min))
            link(dve.tensor_reduce(span[0:ITERS, 1, :], grouped, AX.X, ALU.max))
            link(dve.tensor_copy(span_i[0:ITERS, :], span[0:ITERS, 0, :]))
            link(dve.tensor_tensor(span[0:ITERS, 1, :], span[0:ITERS, 1, :], span[0:ITERS, 0, :], ALU.subtract))
            dve.tensor_reduce(over_f[0:ITERS, :], span[0:ITERS, 1, :], AX.X, ALU.max).then_inc(span_made, 1)

            for n in range(2 * ROWS_IT):
                to, k = (src_i, dst_col)[n // ROWS_IT], n % ROWS_IT
                dve.wait_ge(turned_edges, n + 1)
                dve.tensor_copy(to[:, :, k], turn_ps[n % 2][:, 0:ITERS]).then_inc(kept_edges, 1)
                if n == ROWS_IT:
                    for g in range(GROUPS):
                        dve.tensor_scalar(dst_local[0:ITERS, g * GROUP:(g + 1) * GROUP, :]
                                          .rearrange("p a b -> p (a b)"),
                                          dest_f[0:ITERS, g * GROUP * P:(g + 1) * GROUP * P],
                                          span[0:ITERS, 0, g:g + 1], None, ALU.subtract).then_inc(local_made, 1)
            dve.wait_ge(kept_edges, 2 * ROWS_IT)
            link(dve.tensor_single_scalar(bits_i[:], src_i[:], 7, ALU.logical_shift_right))
            link(dve.tensor_copy(src_tile[:], bits_i[:]))
            link(dve.tensor_single_scalar(bits_i[:], src_i[:], P - 1, ALU.bitwise_and))
            link(dve.tensor_copy(src_node, bits_i[:]))
            dve.wait_ge(base_in, 32)
            link(dve.tensor_reduce(flag_f[:], overs_f[:], AX.X, ALU.max))
            dve.tensor_scalar(flag_i[:], flag_f[:], float(P - 1), None, ALU.is_gt).then_inc(flag_made, 1)
            dve.wait_ge(consts, NCONST)

            def hit(q, row, h):
                dve.tensor_tensor(hits[:, q], src_tile[:, bass.ds(row, 1), h * GROUP:(h + 1) * GROUP]
                                  .to_broadcast([P, NB, GROUP]), tile_row[:], ALU.is_equal).then_inc(hits_made, 1)

            for p in range(NPART):
                first = IT0[p] // 2

                def pair(i, fresh=False):
                    for q in range(4):
                        if not fresh:
                            dve.wait_ge(count_used, dve.snap(i * 4 + (4 * first + q + 1 - 4)))
                        hit(q, i * 2 + (IT0[p] + q // 2), q % 2)

                if p == 0:
                    pair(0, fresh=True)
                    with dve.Fori(1, PARTS[p] // 2) as i:
                        pair(i)
                else:
                    with dve.Fori(0, PARTS[p] // 2) as i:
                        pair(i)
                dve.wait_ge(hist_made, p + 1)
                dve.tensor_reduce(count[:, p, :], hist[:, 0:NT * GROUP].rearrange("p (t c) -> p t c", c=GROUP),
                                  AX.X, ALU.add).then_inc(count_made, 1)
            dve.wait_ge(count_made, NPART)
            link(dve.tensor_copy(count_i[:], count[:]))
            link(dve.tensor_single_scalar(count_i[:], count_i[:], 9, ALU.logical_shift_right))
            link(dve.tensor_scalar(blocks_f[:], count_i[:], 1.0, None, ALU.add))
            for p in range(NPART):
                link(dve.tensor_tensor_scan(block_end[:, p, :], one_row[:], blocks_f[:, p, :], 0.0,
                                            ALU.mult, ALU.add))
            for c in range(2 * NPART):
                link(dve.tensor_scalar(cmp_tile[:, c % 2], block_end[:, c // 2, :], node_col[:, c % 2:c % 2 + 1],
                                       None, ALU.is_le))
                ins = dve.tensor_reduce(tile_of[:, c:c + 1], cmp_tile[:, c % 2], AX.X, ALU.add)
                if c < 2 * NPART - 1:
                    link(ins)
            ins.then_inc(tiles_made, 1)
            for p in range(NPART):
                link(dve.tensor_tensor(base[:, p, 0:NT], block_end[:, p, :], blocks_f[:, p, :], ALU.subtract))
                ins = dve.tensor_scalar(base[:, p, 0:NT], base[:, p, 0:NT], float(J0[p] * BPI), float(BROWS),
                                        ALU.add, ALU.mult)
                link(ins)
                link(dve.tensor_scalar(tail_i[0:1, p * NT:(p + 1) * NT], block_end[0:1, p, :],
                                       float(J0[p] * BPI - 1), None, ALU.add))
            dve.wait_ge(tilerow_made, 1)
            for p in range(NPART):
                link(dve.tensor_copy(tile_f[0:1, J0[p] * BPI:(J0[p] + GITERS[p]) * BPI],
                                     tile_ps[p][:, 0:GITERS[p] * BPI]))
            dve.wait_ge(consts, NCONST + 1)
            link(dve.tensor_copy(tile_i[:], tile_f[0:1]))
            link(dve.tensor_scalar(live_f[0:1], tile_f[0:1], float(NT), None, ALU.is_lt))
            link(dve.tensor_tensor(start_f[0:1], blk_iota[0:1], live_f[0:1], ALU.mult))
            link(dve.tensor_copy(start_i[:], start_f[0:1]))
            dve.sem_inc(tables_made, 1)

            def first_rest(s, made, n, parts):
                dve.wait_ge(proj_made, made)
                dve.wait_ge(high_made, made)
                dve.tensor_tensor(rest[0:n, s, :], proj_ps[s][0:n, :], parts[0:n, 0, :], ALU.subtract
                                  ).then_inc(split_step, 1)

            def second(s, done, n, parts):
                dve.wait_ge(split_step, done)
                dve.tensor_copy(parts[0:n, 1, :], rest[0:n, s, :]).then_inc(split_step, 1)

            def third(s, done, n, parts):
                dve.wait_ge(split_step, done)
                dve.tensor_tensor(parts[0:n, 2, :], rest[0:n, s, :], parts[0:n, 1, :], ALU.subtract
                                  ).then_inc(low_made, 1)

            acc_regs = [dve.alloc_register(f"tile{k}") for k in range(BPI)]

            part = [0]

            def enter(it, j, r, t):
                if it == 0:
                    first_rest(0, FULL_NT + 1, NREST, last3)
                    second(0, 2 * FULL_NT + 1, NREST, last3)
                    third(0, 2 * FULL_NT + 2, NREST, last3)
                if r is not None and 2 * r in IT0:
                    part[0] = IT0.index(2 * r)
                    if part[0]:
                        dve.wait_ge(carry_made, BATCHES * r + part[0])
                    dve.tensor_copy(carry[:, 0], base[:, part[0], :]).then_inc(carry_made, 1)

            def emit(it, j, r, t, drain=False):
                LA = 4
                if it is not None:
                    it1 = plus(dve, it, 1)
                if j is not None:
                    j1 = plus(dve, j, 1)
                    if drain:
                        tiles = words(dve, acc_regs[0:LA], tile_i, j * BPI - LA, NT)
                    elif isinstance(j, int) and j == 0:
                        tiles = [None] * LA + words(dve, acc_regs[LA:BPI], tile_i, 0, NT)
                    else:
                        tiles = words(dve, acc_regs, tile_i, j * BPI - LA, NT)
                def batch(h):
                    return times(dve, r, 2, h // GROUPS)

                def add_totals(h):
                    dve.wait_ge(totals_made, times(dve, r, BATCHES, h + 1))
                    dve.wait_ge(carry_made, times(dve, r, BATCHES, h + part[0] + 1))
                    dve.tensor_tensor(carry[:, (h + 1) % BATCHES], carry[:, h], totals, ALU.add
                                      ).then_inc(carry_made, 1)

                def mask(h):
                    dve.wait_ge(ranks_made, times(dve, r, BATCHES, h + 1))
                    if h >= 2 or not isinstance(r, int) or r:
                        dve.wait_ge(place_made, times(dve, r, BATCHES, h - 1))
                    dve.tensor_tensor(masked[:, h % 2].rearrange("p t c -> p (t c)"), ranks[h % 2],
                                      hits[:, h].rearrange("p t c -> p (t c)"), ALU.mult).then_inc(masked_made, 1)

                def places(h):
                    g = h % GROUPS
                    dve.wait_ge(masked_made, times(dve, r, BATCHES, h + 1))
                    dve.tensor_reduce(place[:, bass.ds(batch(h), 1), g * GROUP:(g + 1) * GROUP]
                                      .rearrange("p a c -> p (a c)"),
                                      masked[:, h % 2].rearrange("p t c -> p c t"), AX.X, ALU.add
                                      ).then_inc(place_made, 1)

                for s in range(STEPS):
                    if r is not None:
                        for h in ((0, 1), (2,), (3,))[s] if s < 3 else ():
                            hit(h, batch(h), h % GROUPS)
                        if 1 <= s <= BATCHES:
                            add_totals(s - 1)
                    if t is not None:
                        if s == 2:
                            for q in range(TSLOT):
                                first_rest(q, times(dve, t, TSLOT, q + 1), P, parts3[:, q])
                        if s == 3:
                            for q in range(TSLOT):
                                second(q, times(dve, t, 2 * TSLOT, q + 1), P, parts3[:, q])
                        if s == 4:
                            for q in range(TSLOT):
                                third(q, times(dve, t, 2 * TSLOT, TSLOT + q + 1), P, parts3[:, q])
                    if j is not None and (at := lagged(s, 1, j, j1, drain)):
                        k, n = at
                        dve.wait_ge(tag_made[k], n)
                        dve.tensor_tensor(hot[:, k], tags[:, k, :].unsqueeze(1).to_broadcast([P, P, BLK]),
                                          node_row[:], ALU.is_equal).then_inc(hot_made[k], 1)
                    if it is not None and s < UNITS:
                        u = s
                        dve.wait_ge(rows_kept[u], it1)
                        slot_free(dve, kv_made[1::2], u, 2, it, it1)
                        dve.tensor_scalar(pick[:, u % 2], dst_rows[:, u % 2], node_col[:, 0:1], None, ALU.is_equal
                                          ).then_inc(pick_made[u], 1)
                    if j is not None:
                        if at := lagged(s, 3, j, j1, drain):
                            k, n = at
                            dve.wait_ge(exp_made[k], n)
                            dve.tensor_tensor(
                                msg[:, k, :, 0:D].rearrange("p b (h f) -> p b h f", h=HEADS),
                                blk[:, k, :, D:2 * D].rearrange("p b (h f) -> p b h f", h=HEADS),
                                msg[:, k, :, D:AW].unsqueeze(3).to_broadcast([P, BLK, HEADS, DH]),
                                ALU.mult).then_inc(msg_made[k], 1)
                        if at := lagged(s, 2, j, j1, drain):
                            k, n = at
                            dve.wait_ge(q_made[k], n)
                            dve.tensor_tensor(qk[:, k], picked_q, blk[:, k, :, 0:D], ALU.mult
                                              ).then_inc(qk_made[k], 1)
                        if at := lagged(s, LA, j, j1, drain):
                            k, n = at
                            dve.wait_ge(sum_made[k], n)
                            one_free(dve, acc_made, k, j, n)
                            now = acc[:, bass.ds(tiles[s], 1), :].rearrange("p a d -> p (a d)")
                            dve.tensor_tensor(now, now, sums, ALU.add).then_inc(acc_made[k], 1)
                    if r is not None:
                        if 2 <= s <= BATCHES + 1:
                            mask(s - 2)
                        if 3 <= s <= BATCHES + 2:
                            places(s - 3)
                    if j is not None and (at := lagged(s, 2, j, j1, drain)):
                        k, n = at
                        dve.wait_ge(qk_made[k], n)
                        dve.tensor_reduce(score[:, k], qk[:, k].rearrange("p b (h f) -> p (b h) f", h=HEADS),
                                          AX.X, ALU.add).then_inc(score_made, 1)
                        dve.wait_ge(score_made, times(dve, j, BPI, k + 1 if s >= 2 else k + 1 - BPI))
                        dve.tensor_scalar(clipped[:, k].rearrange("p b h -> p (b h)"), score[:, k], -CLIP, CLIP,
                                          ALU.max, ALU.min).then_inc(clip_made[k], 1)
                if r is not None:
                    for h in range(STEPS - 3, BATCHES):
                        places(h)

            run(dve, before + rows, emit, enter)
            emit(None, JS, None, None, drain=True)

            dve.wait_ge(acc_made[BPI - 1], JS)
            link(dve.tensor_scalar(inv, acc[:, 0:NT, D:AW], EPS_W, None, ALU.add))
            link(dve.reciprocal(inv, inv))
            dve.wait_ge(loads, 48 + 32)
            for lo, hi in CHUNKS:
                y = acc[:, lo:hi, 0:D]
                y4 = y.rearrange("p t (h f) -> p t h f", h=HEADS)
                link(dve.tensor_tensor(y4, y4, inv[:, lo:hi].unsqueeze(3).to_broadcast([P, hi - lo, HEADS, DH]),
                                        ALU.mult))
                link(dve.scalar_tensor_tensor(y, x_all[:, lo:hi, :], 2.0, y, ALU.mult, ALU.add))
                link(dve.tensor_reduce(stat[:, 0, lo:hi], y, AX.X, ALU.add))
                link(dve.tensor_scalar(stat[:, 1, lo:hi], stat[:, 0, lo:hi], 1.0 / D, None, ALU.mult))
                dve.tensor_tensor(y, y, stat[:, 1, lo:hi].unsqueeze(2).to_broadcast([P, hi - lo, D]),
                                  ALU.subtract).then_inc(centered, 1)
            for c, (lo, hi) in enumerate(CHUNKS):
                dve.wait_ge(square_made, c + 1)
                link(dve.tensor_reduce(stat[:, 0, lo:hi], sq_all[:, lo:hi, :], AX.X, ALU.add))
            dve.tensor_scalar(stat[:, 2, :], stat[:, 0, :], 1.0 / D, EPS_LN, ALU.mult, ALU.add
                              ).then_inc(centered, 1)
            dve.wait_ge(square_made, len(CHUNKS) + 1)
            link(dve.reciprocal(stat[:, 4, :], stat[:, 3, :]))
            for lo, hi in CHUNKS:
                y = acc[:, lo:hi, 0:D]
                dve.tensor_tensor(y, y, stat[:, 4, lo:hi].unsqueeze(2).to_broadcast([P, hi - lo, D]), ALU.mult
                                  ).then_inc(y_made, 1)


_INS = ["x", "src", "dst", "L0_gnn_qW", "L0_gnn_kW", "L0_gnn_vW"]


def kernel(**inputs):
    import numpy as np
    import concourse.bacc as bacc
    from concourse.bass_utils import run_bass_kernel_spmd

    nc = bacc.Bacc("TRN2", target_bir_lowering=False, num_devices=1)
    arrays, args = {}, []
    for name in _INS:
        a = np.ascontiguousarray(inputs[name])
        arrays[f"in_{name}"] = a
        args.append(nc.dram_tensor(f"in_{name}", a.shape, mybir.dt.from_np(a.dtype), kind="ExternalInput").ap())
    x, src, dst, wq, wk, wv = args
    out = nc.dram_tensor("out", arrays["in_x"].shape, F32, kind="ExternalOutput").ap()
    gnn_program(nc, x, src, dst, wq, wk, wv, out)
    r = run_bass_kernel_spmd(nc, [arrays], core_ids=[0])
    return r.results[0]["out"]
```

```python
from contextlib import ExitStack

import concourse.bass as bass
from concourse import mybir

ALU = mybir.AluOpType
ACT = mybir.ActivationFunctionType
AX = mybir.AxisListType
F32 = mybir.dt.float32
BF16 = mybir.dt.bfloat16
I32 = mybir.dt.int32
U32 = mybir.dt.uint32

P = 128
HEADS = 4
CLIP = 10.0
EPS_W = 1e-8
EPS_LN = 1e-5

ROWS_IT = 16
GROUP = 8
UNIT = 4
PARTS = (36, 32, 30)
BPI = 6
TURN = 2
TSLOT = 4
BLK = 4
WROW = 196
TAG = 192


def timetable(parts, gathers, tables):
    start = [sum(parts[:p]) for p in range(len(parts) + 1)]
    gstart = [sum(gathers[:p]) for p in range(len(parts) + 1)]
    pairs = start[-1] // 2
    early = max(tables, pairs - parts[0])
    before = [(None, None, i if i < early else None, i if i < tables else None)
              for i in range(max(early, tables))]
    rows, gather = [], 0
    for p, n in enumerate(parts):
        for i in range(n):
            this = gather if gather < gstart[p] else None
            rank = early + i if p == 0 and early + i < pairs else None
            rows.append((start[p] + i, this, rank, None))
            gather += this is not None
    rows += [(None, j, None, None) for j in range(gather, gstart[-1])]
    return before, rows


def segments(rows, alone, begins):
    runs = []
    for row in rows:
        last = runs[-1][-1] if runs else None
        if (last and not (alone(row) or alone(last) or begins(row))
                and all((a is None) == (b is None) and (a is None or b == a + 1) for a, b in zip(last, row))):
            runs[-1].append(row)
        else:
            runs.append([row])
    return [(r[0], len(r)) for r in runs]


def gnn_program(nc, x, src, dst, wq, wk, wv, out):
    N, D = x.shape
    E = src.shape[0]
    DH = D // HEADS
    NPART = len(PARTS)
    NT = -(-N // P)
    NB = NT + 1
    FULL_NT = N // P
    NREST = N - FULL_NT * P
    NTAB = (NT + 1) * P
    EIT = ROWS_IT * P
    ITERS = sum(PARTS)
    IT0 = [sum(PARTS[:p]) for p in range(NPART)]
    EFULL = E // EIT
    EREST = E - EFULL * EIT
    BROWS = BLK * P
    GITERS = [-(-(n * EIT // BROWS + NT) // BPI) for n in PARTS]
    J0 = [sum(GITERS[:p]) for p in range(NPART)]
    JS = sum(GITERS)
    NBLK = JS * BPI
    SORTED = NBLK * BROWS
    GROUPS = ROWS_IT // GROUP
    BATCHES = 2 * GROUPS
    UNITS = ROWS_IT // UNIT
    PAIRS = ROWS_IT // 2
    KVS = 3
    STEPS = max(BPI, UNITS + 2, BATCHES + 2)
    FAR = 1 << 20
    AW = D + HEADS
    assert ITERS == -(-E // EIT) <= P and all(n % 2 == 0 for n in PARTS)
    assert SORTED < FAR and FULL_NT % TSLOT == 0 and NT == FULL_NT + 1
    TURNS = -(-NT // TURN)
    assert all(n >= TURNS for n in PARTS[:-1])
    assert max(GITERS) * BPI <= 2 * P and GROUPS == 2 and UNITS == 4 and STEPS >= 5

    CHUNKS = [(NT * c // 4, NT * (c + 1) // 4) for c in range(4)]

    TI = FULL_NT // TSLOT
    before, rows = timetable(PARTS, GITERS, TI)

    kv3 = nc.dram_tensor("kv3_table", (NTAB, 3 * 2 * D), BF16).ap()
    rows_dram = nc.dram_tensor("sorted_rows", (SORTED, WROW), F32).ap()
    base_tmp = nc.dram_tensor("base_tmp", (ITERS, GROUPS), I32).ap()
    over_tmp = nc.dram_tensor("over_tmp", (ITERS, 1), F32).ap()

    with ExitStack() as ctx:
        def sb(name, shape, dt):
            return ctx.enter_context(nc.sbuf_tensor(name, shape, dt))

        def sem(name):
            return ctx.enter_context(nc.semaphore(name))

        def sems(name, n):
            return [sem(f"{name}{i}") for i in range(n)]

        ident_f = sb("ident_f", [P, P], F32)
        ident_b = sb("ident_b", [P, P], BF16)
        ones_b = sb("ones_b", [P, P], BF16)
        below_b = sb("below_b", [P, P], BF16)
        zeros_b = sb("zeros_b", [P, 3 * 2 * D], BF16)
        node_col = sb("node_col", [P, 2], F32)
        node_row = sb("node_row", [P, P, BLK], BF16)
        tile_row = sb("tile_row", [P, NB, GROUP], BF16)
        one_row = sb("one_row", [P, NT], F32)
        pad_rows = sb("pad_rows", [P, BLK, WROW], F32)
        weights = sb("weights", [D, 3 * D], F32)
        q3 = sb("q3", [P, NT + 1, 3, D], BF16)
        acc = sb("acc", [P, NT + 1, AW], F32)
        src_i = sb("src_i", [P, ITERS, ROWS_IT], I32)
        bits_i = sb("bits_i", [P, ITERS, ROWS_IT], I32)
        place = bits_i[:].bitcast(F32)
        src_tile = sb("src_tile", [P, ITERS, ROWS_IT], BF16)
        src_node = src_i[:].bitcast(F32)
        dst_col = sb("dst_col", [P, ITERS, ROWS_IT], I32)
        dst_local = sb("dst_local", [P, ROWS_IT, P], BF16)
        last3 = sb("last3", [P, 3, 3 * D], BF16)
        window = sb("window", [P, GROUPS, 3, 2 * D], BF16)
        dst_rows = sb("dst_rows", [P, 2, UNIT * P], BF16)
        pick = sb("pick", [P, 2, UNIT * P], BF16)
        FAR_WORDS = GROUP * 3 * 2 * D // 2
        spread_space = sb("spread_space", [P, FAR_WORDS + ROWS_IT * WROW], F32)
        payload = spread_space[:, FAR_WORDS:].rearrange("p (k w) -> p k w", k=ROWS_IT)
        place_now = sb("place_now", [P, ROWS_IT], U32)
        dst_now = sb("dst_now", [P, GROUP], U32)
        far_rows = (spread_space[:, 0:FAR_WORDS].bitcast(BF16)
                    .rearrange("p (k a d) -> p k a d", k=GROUP, a=3))
        x_all = spread_space[:, 0:NT * D].rearrange("p (t d) -> p t d", t=NT)
        hits = sb("hits", [P, BATCHES, NB, GROUP], BF16)
        masked = sb("masked", [P, 2, NB, GROUP], F32)
        carry = sb("carry", [P, BATCHES, NB], F32)
        count = sb("count", [P, NPART, NT], F32)
        count_i = sb("count_i", [P, NPART, NT], I32)
        blocks_f = sb("blocks_f", [P, NPART, NT], F32)
        block_end = sb("block_end", [P, NPART, NT], F32)
        base = sb("base", [P, NPART, NB], F32)
        cmp_tile = sb("cmp_tile", [P, 2, NT], F32)
        tile_of = sb("tile_of", [P, 2 * NPART], F32)
        tail_i = sb("tail_i", [1, NPART * NT], I32)
        tile_i = sb("tile_i", [1, NBLK + BPI], I32)
        start_i = sb("start_i", [1, NBLK], I32)
        span = sb("span", [P, 2, GROUPS], F32)
        over_f = sb("over_f", [P, 1], F32)
        span_i = sb("span_i", [P, GROUPS], I32)
        base_i = sb("base_i", [1, ITERS * GROUPS], I32)
        overs_f = sb("overs_f", [1, ITERS], F32)
        flag_f = sb("flag_f", [1, 1], F32)
        flag_i = sb("flag_i", [1, 1], I32)
        WORK = 19000
        work = sb("work", [P, WORK], F32)

        def share(at, shape, dt):
            n = 1
            for d in shape:
                n *= d
            words = n // 2 if dt == BF16 else n
            assert at + words <= WORK
            v = work[:, at:at + words]
            v = v if dt == F32 else v.bitcast(dt)
            if len(shape) == 1:
                return v, at + words
            names = " ".join(f"d{i}" for i in range(len(shape)))
            return v.rearrange(f"p ({names}) -> p {names}",
                               **{f"d{i}": d for i, d in enumerate(shape)}), at + words

        edge_i, at = share(0, [EIT], I32)
        edge_f, at = share(at, [EIT], F32)
        dest_i, at = share(at, [EIT], I32)
        dest_f, at = share(at, [EIT], F32)
        x_in, at = share(at, [TSLOT, D], F32)
        xT, at = share(at, [TSLOT, P], F32)
        parts3, at = share(at, [TSLOT, 3, 3 * D], BF16)
        rest, at = share(at, [TSLOT, 3 * D], F32)
        blk_iota, at = share(0, [NBLK], F32)
        tile_f, at = share(at, [NBLK], F32)
        live_f, at = share(at, [NBLK], F32)
        start_f, at = share(at, [NBLK], F32)
        blk, at = share(0, [BPI, 2, BLK, WROW], F32)
        tags, at = share(at, [BPI, BLK], BF16)
        hot, at = share(at, [BPI, P, BLK], BF16)
        hot_f, at = share(at, [BPI, BLK, P], F32)
        hot_T, at = share(at, [BPI, BLK, P], BF16)
        qk, at = share(at, [2, BLK, D], F32)
        score, at = share(at, [BPI, BLK * HEADS], F32)
        clipped, at = share(at, [BPI, BLK, HEADS], F32)
        msg, at = share(at, [BPI, BLK, AW], F32)
        sq_all, at = share(0, [NT, D], F32)
        inv, at = share(at, [NT, HEADS], F32)
        stat, at = share(at, [5, NT], F32)

        def ps(name, shape):
            return ctx.enter_context(nc.psum_tensor(name, shape, F32))

        rows_bank = ps("rows_bank", [P, 512])
        kv_bank = [ps(f"kv_bank{i}", [P, 512]) for i in range(KVS)]
        q_bank = ps("q_bank", [P, 512])
        turn_bank = ps("turn_bank", [P, 512])
        sum_bank = ps("sum_bank", [P, 512])
        rank_bank = ps("rank_bank", [P, 512])
        turned = turn_bank[:, 0:BLK * P // 2].bitcast(BF16).rearrange("p (b n) -> p b n", b=BLK)
        sums = sum_bank[:, 0:AW]
        picked_q = q_bank[:, 0:BLK * D].rearrange("p (b d) -> p b d", b=BLK)
        ranks = [b[:, 0:NB * GROUP] for b in (rank_bank, q_bank)]
        totals = sum_bank[:, 0:NB]
        hist = q_bank[:, 0:NB * GROUP]
        xT_ps = rows_bank[0:D, 0:TSLOT * P].rearrange("p (s n) -> p s n", s=TSLOT)
        proj_ps = [b[:, 0:3 * D] for b in (*kv_bank, turn_bank)]
        turn_ps = [b[:, 0:P] for b in (rows_bank, rank_bank)]
        tile_ps = [b[0:1, h * 2 * P:(h + 1) * 2 * P] for b in (rows_bank, rank_bank) for h in range(2)]

        consts = sem("consts")
        loads = sem("loads")
        edge_pads = sem("edge_pads")
        edges_in = sem("edges_in")
        edges_f = sem("edges_f")
        turned_edges = sem("turned_edges")
        kept_edges = sem("kept_edges")
        dve_step = sem("dve_step")
        span_made = sem("span_made")
        span_out = sem("span_out")
        base_in = sem("base_in")
        local_made = sem("local_made")
        flag_made = sem("flag_made")
        x_loaded = sem("x_loaded")
        xT_made = sem("xT_made")
        xT_kept = sem("xT_kept")
        proj_made = sem("proj_made")
        high_made = sem("high_made")
        split_step = sem("split_step")
        low_made = sem("low_made")
        q_kept = sem("q_kept")
        table_out = sem("table_out")
        rest_out = sem("rest_out")
        hits_made = sem("hits_made")
        count_used = sem("count_used")
        hist_made = sem("hist_made")
        count_made = sem("count_made")
        tiles_made = sem("tiles_made")
        tilerow_made = sem("tilerow_made")
        tables_made = sem("tables_made")
        totals_made = sem("totals_made")
        carry_made = sem("carry_made")
        ranks_made = sem("ranks_made")
        masked_made = sem("masked_made")
        place_made = sem("place_made")
        tails_out = sems("tails_out", NPART)
        window_in = sems("window_in", GROUPS)
        spread_rows = sems("spread_rows", UNITS)
        rows_kept = sems("rows_kept", UNITS)
        pick_made = sems("pick_made", UNITS)
        kv_made = sems("kv_made", PAIRS)
        payload_made = sems("payload_made", PAIRS)
        tags_made = sems("tags_made", GROUPS)
        scattered = sems("scattered", UNITS)
        slow_step = sem("slow_step")
        fetched = sem("fetched")
        pool_turn = sem("pool_turn")
        blk_in = sems("blk_in", BPI)
        tag_made = sems("tag_made", BPI)
        hot_made = sems("hot_made", BPI)
        turned_made = sems("turned_made", BPI)
        hotT_made = sems("hotT_made", BPI)
        q_made = sems("q_made", BPI)
        qk_made = sems("qk_made", BPI)
        score_made = sem("score_made")
        clip_made = sems("clip_made", BPI)
        exp_made = sems("exp_made", BPI)
        msg_made = sems("msg_made", BPI)
        sum_made = sems("sum_made", BPI)
        acc_made = sems("acc_made", BPI)
        square_made = sem("square_made")
        centered = sem("centered")
        y_made = sem("y_made")
        stored = sem("stored")

        NCONST = 20

        def lagged(s, lag, j, j1, drain=False):
            if s >= lag:
                return None if drain or s - lag >= BPI else (s - lag, j1)
            return None if isinstance(j, int) and j == 0 else (s - lag + BPI, j)

        def one_free(eng, sem_list, k, j, j1):
            if k:
                eng.wait_ge(sem_list[k - 1], j1)
            elif not (isinstance(j, int) and j == 0):
                eng.wait_ge(sem_list[-1], j)

        def slot_free(eng, sem_list, n, slots, it, it1):
            if n >= slots:
                eng.wait_ge(sem_list[n - slots], it1)
            elif not (isinstance(it, int) and it == 0):
                eng.wait_ge(sem_list[max(m for m in range(len(sem_list)) if m % slots == n)], it)

        def plus(eng, v, by):
            return v + by if isinstance(v, int) else eng.snap(v + by)

        def times(eng, v, by, more=0):
            return v * by + more if isinstance(v, int) else eng.snap(v * by + more)

        def loop(eng, n, emit):
            emit(0)
            with eng.Fori(0, n - 1) as i:
                emit(eng.snap(i + 1))

        COUNTED = ITERS * GROUPS

        LAST_PAIR = ITERS // 2 - 1

        def alone(row):
            return 0 in row or row[2] == LAST_PAIR

        def begins(row):
            return row[0] in IT0 or row[1] in J0 or (row[2] is not None and 2 * row[2] in IT0)

        def run(eng, rows, emit, enter=None, begins=begins):
            for first, n in segments(rows, alone, begins):
                if enter:
                    enter(*first)
                if n == 1:
                    emit(*first)
                else:
                    with eng.Fori(0, n) as i:
                        emit(*(None if v is None else eng.snap(i + v) for v in first))

        def words(eng, regs, table, at, top):
            eng.reg_load(regs, table[0:1, bass.ds(at, len(regs))])
            return [eng.snap(x, min_val=0, max_val=top) for x in regs]

        def first_tiles(eng, regs, lag):
            eng.reg_load(regs[lag:], tile_i[0:1, 0:BPI - lag])

        def next_tiles(eng, regs, j, lag):
            eng.reg_load(regs, tile_i[0:1, bass.ds(times(eng, j, BPI, BPI - lag), BPI)])

        def halves_of(eng, j):
            return (j & 1, (j + 1) & 1) if isinstance(j, int) else (eng.snap(j & 1), eng.snap((j + 1) & 1))

        def held(k, late, halves, cols):
            return blk[:, k, bass.ds(halves[late], 1), :, cols].rearrange("p o b w -> p (o b) w")

        def weigh(eng, k, n, late, halves):
            eng.wait_ge(exp_made[k], n)
            eng.tensor_tensor(
                msg[:, k, :, 0:D].rearrange("p b (h f) -> p b h f", h=HEADS),
                held(k, late, halves, slice(D, 2 * D)).rearrange("p b (h f) -> p b h f", h=HEADS),
                msg[:, k, :, D:AW].unsqueeze(3).to_broadcast([P, BLK, HEADS, DH]),
                ALU.mult).then_inc(msg_made[k], 1)

        block = ctx.enter_context(nc.Block())

        @block.gpsimd
        def _(pool):
            pool.memset(ident_f[:], 0.0).then_inc(consts, 1)
            pool.memset(ident_b[:], 0.0).then_inc(consts, 1)
            pool.memset(below_b[:], 1.0).then_inc(consts, 1)
            pool.wait_ge(consts, 3)
            for m in (ident_f, ident_b):
                pool.affine_select(out=m[:], in_=m[:], compare_op=ALU.not_equal, fill=1.0, base=0,
                                   pattern=[[-1, P]], channel_multiplier=1).then_inc(consts, 1)
            pool.affine_select(out=below_b[:], in_=below_b[:], compare_op=ALU.is_gt, fill=0.0, base=0,
                               pattern=[[1, P]], channel_multiplier=-1).then_inc(consts, 1)
            pool.memset(last3[:], 0.0).then_inc(consts, 1)
            pool.memset(q3[:, FULL_NT:NT + 1], 0.0).then_inc(consts, 1)
            for held, pattern, by in ((node_col, [[P, 2]], 1), (node_row, [[1, P], [0, BLK]], 0),
                                      (tile_row, [[1, NB], [0, GROUP]], 0)):
                pool.iota(held[:], pattern, base=0, channel_multiplier=by,
                          allow_small_or_imprecise_dtypes=True).then_inc(consts, 1)
            pool.memset(pad_rows[:], 0.0).then_inc(consts, 1)
            pool.wait_ge(consts, 12)
            pool.memset(pad_rows[:, :, TAG:TAG + 1], -1.0).then_inc(consts, 1)
            pool.memset(ones_b[:], 1.0).then_inc(consts, 1)
            pool.memset(zeros_b[:], 0.0).then_inc(consts, 1)
            pool.memset(one_row[:], 1.0).then_inc(consts, 1)
            pool.memset(acc[:], 0.0).then_inc(consts, 1)
            pool.memset(payload[:, :, TAG:WROW], 0.0).then_inc(consts, 1)
            pool.memset(base[:, :, NT:NB], float(FAR)).then_inc(consts, 1)
            pool.memset(tile_i[:], 0).then_inc(consts, 1)
            pool.wait_ge(kept_edges, 2 * ROWS_IT)
            pool.iota(blk_iota[0:1, :], [[1, NBLK]], base=0, channel_multiplier=0,
                      allow_small_or_imprecise_dtypes=True).then_inc(consts, 1)

            pool.wait_ge(flag_made, 1)
            over = pool.value_load(flag_i[0:1, 0:1], min_val=0, max_val=1)
            pool.wait_ge(table_out, 16 * FULL_NT)
            pool.wait_ge(rest_out, 32)
            last_place = pool.to_reg(SORTED - 1)
            last_row = pool.to_reg(NTAB - 1)

            def scatter(u, it1):
                pool.wait_ge(payload_made[2 * u + 1], it1)
                pool.sem_inc(pool_turn, 1)
                for k in range(UNIT * u, UNIT * (u + 1)):
                    pool.indirect_dma_start(
                        out=rows_dram, out_offset=bass.IndirectOffsetOnAxis(ap=place_now[:, k:k + 1], axis=0),
                        in_=payload[:, k, :], in_offset=None,
                        bounds_check=last_place, oob_is_err=False).then_inc(scattered[u], 16)

            def fast(it):
                it1 = pool.snap(it + 1)
                it2 = pool.snap(it * 2 + 2)
                for u in range(UNITS):
                    if u % 2 == 0:
                        pool.wait_ge(tags_made[u // 2], it2)
                    scatter(u, it1)

            COUNTS = 3

            def slow(it):
                it1 = pool.snap(it + 1)
                it2 = pool.snap(it * 2 + 2)
                for g in range(GROUPS):
                    copied, added, summed = (
                        pool.snap(it * (GROUPS * COUNTS) + (g * COUNTS + n)) for n in (1, 2, 3))
                    gathered = pool.snap(it * (GROUPS * GROUP * 16) + (g + 1) * GROUP * 16)
                    for u in range(2 * g, 2 * g + 2):
                        pool.wait_ge(payload_made[2 * u + 1], it1)
                    pool.wait_ge(tags_made[g], it2)
                    pool.tensor_copy(dst_now[:], dst_col[:, bass.ds(it, 1), g * GROUP:(g + 1) * GROUP]
                                     .rearrange("p a b -> p (a b)")).then_inc(slow_step, 1)
                    pool.wait_ge(slow_step, copied)
                    pool.sem_inc(pool_turn, 1)
                    for k in range(GROUP):
                        pool.indirect_dma_start(
                            out=far_rows[:, k].rearrange("p a b -> p (a b)"), out_offset=None,
                            in_=kv3, in_offset=bass.IndirectOffsetOnAxis(ap=dst_now[:, k:k + 1], axis=0),
                            bounds_check=last_row, oob_is_err=False).then_inc(fetched, 16)
                    to = payload[:, g * GROUP:(g + 1) * GROUP, 0:2 * D]
                    pool.wait_ge(fetched, gathered)
                    pool.tensor_tensor(to, far_rows[:, :, 0, :], far_rows[:, :, 1, :], ALU.add
                                       ).then_inc(slow_step, 1)
                    pool.wait_ge(slow_step, added)
                    pool.tensor_tensor(to, to, far_rows[:, :, 2, :], ALU.add).then_inc(slow_step, 1)
                    pool.wait_ge(slow_step, summed)
                    for u in range(2 * g, 2 * g + 2):
                        scatter(u, it1)

            def spread(one):
                for p in range(NPART):
                    pool.wait_ge(tails_out[p], 16 * NT)
                    with pool.Fori(IT0[p], IT0[p] + PARTS[p]) as it:
                        one(it)

            with pool.If(over == 0):
                spread(fast)
            with pool.Else():
                spread(slow)

            def emit(it, j, r, t, drain=False):
                j1, halves = plus(pool, j, 1), halves_of(pool, j)
                for s in range(STEPS):
                    if at := lagged(s, 4, j, j1, drain):
                        weigh(pool, *at, s < 4, halves)

            run(pool, [row for row in rows if row[0] is None], emit)
            emit(None, JS, None, None, drain=True)

        @block.sync
        def _(sp):
            sp.wait_ge(edge_pads, 2)
            for flat, held in ((src, edge_i), (dst, dest_i)):
                sp.dma_start(held[0:EFULL, :], flat[0:EFULL * EIT].rearrange("(i e) -> i e", e=EIT)
                             ).then_inc(edges_in, 16)
                sp.dma_start(held[EFULL:EFULL + 1, 0:EREST],
                             flat[EFULL * EIT:E].rearrange("(i e) -> i e", i=1)).then_inc(edges_in, 16)
            for n, w in enumerate((wk, wv, wq)):
                sp.dma_start(weights[:, n * D:(n + 1) * D], w).then_inc(loads, 16)

            tail_regs = [sp.alloc_register(f"tail{k}") for k in range(max(TURN, TSLOT))]
            lo_regs = [sp.alloc_register(f"window{g}") for g in range(GROUPS)]
            half_reg, before_reg = sp.alloc_register("half"), sp.alloc_register("before")
            start_regs = [sp.alloc_register(f"start{k}") for k in range(BPI)]
            rows_of_block = rows_dram.rearrange("(b p k) w -> b p k w", p=P, k=BLK)

            def of_block(b):
                return rows_of_block[bass.ds(b, 1)].rearrange("b p k w -> (b p) k w")

            def table_rows(at, parts, done):
                sp.dma_start(kv3[at, :].rearrange("p (a b) -> p a b", a=3), parts[:, :, 0:2 * D]
                             ).then_inc(done, 16)

            def outs(j):
                for s in range(TSLOT):
                    sp.wait_ge(low_made, times(sp, j, TSLOT, s + 1))
                    table_rows(bass.ds(j * (TSLOT * P) + s * P, P), parts3[:, s], table_out)

            def features(j):
                for s in range(TSLOT):
                    if not isinstance(j, int):
                        sp.wait_ge(xT_made, j)
                    sp.dma_start(x_in[:, s, :], x[bass.ds(j * (TSLOT * P) + s * P, P), :]
                                 ).then_inc(x_loaded, 16)
                if not isinstance(j, int):
                    outs(sp.snap(j - 1))

            def pad_tails(at, regs, p):
                for b in words(sp, regs, tail_i, at, NBLK - 1):
                    sp.dma_start(of_block(b), pad_rows[:]).then_inc(tails_out[p], 16)

            def features_and_tails(j):
                features(j)
                if isinstance(j, int):
                    sp.wait_ge(consts, NCONST)
                    sp.wait_ge(tables_made, 1)
                pad_tails(times(sp, j, TSLOT), tail_regs[0:TSLOT], 0)

            loop(sp, TI, features_and_tails)
            pad_tails(FULL_NT, tail_regs[0:1], 0)
            sp.wait_ge(xT_made, TI)
            sp.dma_start(x_in[0:NREST, 0, :], x[FULL_NT * P:N, :]).then_inc(x_loaded, 16)
            outs(TI - 1)
            sp.wait_ge(low_made, FULL_NT + 1)
            table_rows(slice(FULL_NT * P, NT * P), last3, rest_out)
            sp.wait_ge(consts, NCONST)
            sp.dma_start(kv3[NT * P:NTAB, :], zeros_b[:]).then_inc(rest_out, 16)

            def with_tails(row):
                it, j, *_ = row
                if it is None:
                    return it, j, None
                p = max(q for q in range(NPART) if IT0[q] <= it)
                n = it - IT0[p]
                return it, j, (p + 1) * TURNS + n if p + 1 < NPART and n < TURNS else None

            sp.wait_ge(table_out, 16 * FULL_NT)
            sp.wait_ge(rest_out, 32)
            sp.wait_ge(base_in, 32)
            part = [0]

            X_AT = J0[-1] + 4

            def enter(it, j, n):
                if j == X_AT:
                    sp.dma_start(x_all[:, 0:FULL_NT, :], x[0:FULL_NT * P, :].rearrange("(t p) d -> p t d", p=P)
                                 ).then_inc(loads, 16)
                    sp.dma_start(x_all[0:NREST, FULL_NT, :], x[FULL_NT * P:N, :]).then_inc(loads, 16)
                if n is not None:
                    part[0] = n // TURNS
                if j in J0:
                    p = J0.index(j)
                    for u in range(UNITS):
                        sp.wait_ge(scattered[u], 16 * UNIT * (IT0[p] + PARTS[p]))

            def emit(it, j, n):
                def window_of(g, lo):
                    if not (isinstance(it, int) and it == 0):
                        sp.wait_ge(kv_made[4 * g + 3], it)
                    sp.dma_start(window[:, g].rearrange("p a b -> p (a b)"), kv3[bass.ds(lo, P), :]
                                 ).then_inc(window_in[g], 16)

                def load(k):
                    if not (isinstance(j, int) and j == 0):
                        sp.wait_ge(tag_made[k], j)
                        if not (isinstance(j, int) and j == 1):
                            sp.wait_ge(msg_made[k], j1)
                    sp.dma_start(blk[:, k, bass.ds(half, 1)].rearrange("p o b w -> p (o b) w"), of_block(starts[k])
                                 ).then_inc(blk_in[k], 16)

                if j is not None:
                    half, j1 = j & 1, j - 1
                    if not isinstance(j, int):
                        sp.reg_mov(half_reg, half)
                        sp.reg_mov(before_reg, j1)
                        half = sp.snap(half_reg, min_val=0, max_val=1)
                        j1 = sp.snap(before_reg, min_val=1, max_val=JS)
                    starts = words(sp, start_regs, start_i, j * BPI, NBLK - 1)
                    for k in range(BPI - 2):
                        load(k)
                if it is not None:
                    los = words(sp, lo_regs, base_i, it * GROUPS, N - 1)
                    window_of(0, los[0])
                if j is not None:
                    for k in range(BPI - 2, BPI):
                        load(k)
                if it is not None:
                    window_of(1, los[1])
                if n is not None:
                    p = part[0]
                    few = NT - (TURNS - 1) * TURN if isinstance(n, int) and n % TURNS == TURNS - 1 else TURN
                    pad_tails(times(sp, n, TURN, p * (NT - TURNS * TURN)), tail_regs[0:few], p)

            sp_rows = [with_tails(row) for row in rows]
            run(sp, sp_rows, emit, enter,
                begins=lambda row: (row[0] in IT0 or row[1] in (*J0, 1, 2, X_AT)
                                    or (row[2] is not None and row[2] % TURNS in (0, TURNS - 1))))

            for c, (lo, hi) in enumerate(CHUNKS):
                sp.wait_ge(y_made, c + 1)
                full = min(hi, FULL_NT)
                sp.dma_start(out[lo * P:full * P, :].rearrange("(t p) d -> p t d", p=P),
                             acc[:, lo:full, 0:D]).then_inc(stored, 16)
                if hi == NT:
                    sp.dma_start(out[FULL_NT * P:N, :], acc[0:NREST, FULL_NT, 0:D]).then_inc(stored, 16)
            sp.wait_ge(stored, 16 * (len(CHUNKS) + 1))

        @block.scalar
        def _(act):
            act.wait_ge(span_made, 1)
            act.dma_start(base_tmp, span_i[0:ITERS, :]).then_inc(span_out, 16)
            act.dma_start(over_tmp, over_f[0:ITERS, :]).then_inc(span_out, 16)
            act.wait_ge(span_out, 32)
            act.dma_start(base_i[:], base_tmp.rearrange("(o a) b -> o (a b)", o=1)).then_inc(base_in, 16)
            act.dma_start(overs_f[:], over_tmp.rearrange("(o a) b -> o (a b)", o=1)).then_inc(base_in, 16)
            act.wait_ge(consts, NCONST)

            def high(s, j, n, parts):
                act.wait_ge(proj_made, times(act, j, TSLOT, s + 1))
                act.activation(parts[0:n, 0, :], proj_ps[s][0:n, :], ACT.Copy).then_inc(high_made, 1)

            def keep_q(s, j, n, parts, to):
                act.wait_ge(low_made, times(act, j, TSLOT, s + 1))
                act.activation(to, parts[0:n, :, 2 * D:3 * D], ACT.Copy).then_inc(q_kept, 1)

            def enter(it, j, r, t):
                if it == 0:
                    act.wait_ge(xT_made, TI + 1)
                    act.activation(xT[0:D, 0, 0:NREST], xT_ps[:, 0, 0:NREST], ACT.Copy).then_inc(xT_kept, 1)
                    high(0, TI, NREST, last3)
                    keep_q(0, TI, NREST, last3, q3[0:NREST, FULL_NT])

            def emit(it, j, r, t, drain=False):
                if it is not None:
                    it1, it64 = plus(act, it, 1), times(act, it, 16 * UNIT)
                    here = bass.ds(it, 1)
                if j is not None:
                    j1, j16 = plus(act, j, 1), times(act, j, 16, 16)
                    halves = halves_of(act, j)

                for s in range(STEPS):
                    if t is not None:
                        if s == 1:
                            act.wait_ge(xT_made, plus(act, t, 1))
                            act.activation(xT[0:D], xT_ps, ACT.Copy).then_inc(xT_kept, 1)
                        if s == 2:
                            if not isinstance(t, int):
                                act.wait_ge(table_out, times(act, t, 16 * TSLOT))
                            for q in range(TSLOT):
                                high(q, t, P, parts3[:, q])
                        if s == 4:
                            for q in range(TSLOT):
                                keep_q(q, t, P, parts3[:, q],
                                       q3[:, bass.ds(times(act, t, TSLOT, q), 1), :, :].rearrange("p o a d -> p (o a) d"))
                    if j is not None:
                        if at := lagged(s, 0, j, j1, drain):
                            k, n = at
                            act.wait_ge(blk_in[k], j16)
                            act.activation(tags[:, k, :].unsqueeze(2), held(k, 0, halves, slice(TAG, TAG + 1)), ACT.Copy
                                           ).then_inc(tag_made[k], 1)
                        if at := lagged(s, 4, j, j1, drain):
                            k, n = at
                            act.wait_ge(clip_made[k], n)
                            act.activation(msg[:, k, :, D:AW], clipped[:, k], ACT.Exp).then_inc(exp_made[k], 1)
                    if it is not None and s in (1, 3):
                        g = s // 2
                        cols = slice(g * GROUP, (g + 1) * GROUP)
                        act.wait_ge(place_made, times(act, it, GROUPS, g + 1))
                        if not (isinstance(it, int) and it == 0):
                            act.wait_ge(scattered[2 * g], it64)
                            act.wait_ge(scattered[2 * g + 1], it64)
                        act.activation(place_now[:, cols], place[:, here, cols].rearrange("p a b -> p (a b)"),
                                       ACT.Copy).then_inc(tags_made[g], 1)
                        act.activation(payload[:, cols, TAG:TAG + 1].rearrange("p a b -> p (a b)"),
                                       src_node[:, here, cols].rearrange("p a b -> p (a b)"), ACT.Copy
                                       ).then_inc(tags_made[g], 1)
                    if j is not None:
                        if at := lagged(s, 2, j, j1, drain):
                            k, n = at
                            act.wait_ge(turned_made[k], n)
                            act.activation(hot_T[:, k], turned, ACT.Copy).then_inc(hotT_made[k], 1)
                        if at := lagged(s, 2, j, j1, drain):
                            k, n = at
                            act.wait_ge(hot_made[k], n)
                            act.activation(hot_f[:, k], hot[:, k].rearrange("p n b -> p b n"), ACT.Copy)
                    if it is not None and 2 <= s <= UNITS + 1:
                        for n in (2 * s - 4, 2 * s - 3):
                            act.wait_ge(kv_made[n], it1)
                            act.activation(payload[:, 2 * n:2 * n + 2, 0:2 * D],
                                           kv_bank[n % KVS][:, 0:4 * D].rearrange("p (b d) -> p b d", b=2),
                                           ACT.Copy).then_inc(payload_made[n], 1)
                    if it is not None and s < UNITS:
                        act.wait_ge(spread_rows[s], it1)
                        slot_free(act, pick_made, s, 2, it, it1)
                        act.activation(dst_rows[:, s % 2], rows_bank[:], ACT.Copy).then_inc(rows_kept[s], 1)

            run(act, before + rows, emit, enter)
            emit(None, JS, None, None, drain=True)

            for c, (lo, hi) in enumerate(CHUNKS):
                act.wait_ge(centered, c + 1)
                act.activation(sq_all[:, lo:hi, :], acc[:, lo:hi, 0:D], ACT.Square).then_inc(square_made, 1)
            act.wait_ge(centered, len(CHUNKS) + 1)
            act.activation(stat[:, 3, :], stat[:, 2, :], ACT.Sqrt).then_inc(square_made, 1)

        @block.tensor
        def _(pe):
            pe.wait_ge(consts, NCONST)
            pe.wait_ge(edges_f, 2)
            for n in range(2 * ROWS_IT):
                held, k = (edge_f, dest_f)[n // ROWS_IT], n % ROWS_IT
                if n >= 2:
                    pe.wait_ge(kept_edges, n - 1)
                pe.transpose(turn_ps[n % 2][:, 0:ITERS], held[0:ITERS, k * P:(k + 1) * P],
                             ident_f[0:ITERS, 0:ITERS]).then_inc(turned_edges, 1)
            pe.wait_ge(kept_edges, 2 * ROWS_IT)

            pairs = [0]
            for p in range(NPART):
                if p:
                    pe.wait_ge(count_made, p)
                pe.matmul(hist, ones_b[:], zeros_b[:, 0:NB * GROUP], start=True, stop=False)
                with pe.Fori(0, PARTS[p] // 2) as i:
                    for q in range(2):
                        pe.wait_ge(hits_made, pe.snap(i * 4 + (4 * pairs[0] + 2 * q + 2)))
                        for h in range(GROUPS):
                            mm = pe.matmul(hist, ones_b[:], hits[:, GROUPS * q + h].rearrange("p t c -> p (t c)"),
                                           start=False, stop=False)
                        mm.then_inc(count_used, 1)
                pairs[0] += PARTS[p] // 2
                pe.matmul(hist, ones_b[:], zeros_b[:, 0:NB * GROUP], start=False, stop=True
                          ).then_inc(hist_made, 1)

            pe.wait_ge(tiles_made, 1)
            for c in range(2 * NPART):
                mm = pe.matmul(tile_ps[c // 2][:, (c % 2) * P:(c % 2 + 1) * P], tile_of[:, c:c + 1], ident_f[:],
                               start=True, stop=True)
            mm.then_inc(tilerow_made, 1)
            pe.wait_ge(tables_made, 1)

            pe.wait_ge(loads, 48)

            def turn(s, n, last):
                mm = pe.transpose(xT_ps[:, s, 0:n], x_in[0:n, s, :], ident_f[0:n, 0:n])
                if last:
                    mm.then_inc(xT_made, 1)

            def project(s, j, n):
                if not (isinstance(j, int) and j == 0):
                    pe.wait_ge(split_step, times(pe, j, 2 * TSLOT, s + 1 - 2 * TSLOT))
                pe.matmul(proj_ps[s][0:n, :], xT[0:D, s, 0:n], weights[:], start=True, stop=True
                          ).then_inc(proj_made, 1)

            pe.wait_ge(local_made, GROUPS)
            LQ = 3
            tile_regs = [pe.alloc_register(f"tile{k}") for k in range(BPI)]

            part = [0]

            def enter(it, j, r, t):
                if r is not None and 2 * r in IT0:
                    part[0] = IT0.index(2 * r)
                if it == 0:
                    pe.wait_ge(xT_kept, TI)
                    pe.wait_ge(x_loaded, 16 * (FULL_NT + 1))
                    turn(0, NREST, True)
                    pe.wait_ge(xT_kept, TI + 1)
                    project(0, TI, NREST)
                    pe.wait_ge(split_step, 2 * FULL_NT + 2)
                    pe.wait_ge(q_kept, FULL_NT + 1)
                if j == 0:
                    pe.wait_ge(masked_made, ITERS * GROUPS)
                    pe.wait_ge(carry_made, ITERS * GROUPS + NPART)
                    first_tiles(pe, tile_regs, LQ)

            def emit(it, j, r, t, drain=False):
                if it is not None:
                    it1, it16 = plus(pe, it, 1), times(pe, it, 16, 16)
                    sel = ident_b[0:ITERS, bass.ds(it, 1)].to_broadcast([ITERS, P])
                if j is not None:
                    j1 = plus(pe, j, 1)
                def total(h):
                    pe.wait_ge(hits_made, times(pe, r, BATCHES, COUNTED + h + 1))
                    pe.wait_ge(carry_made, times(pe, r, BATCHES, h + part[0] + 1))
                    for c in range(GROUP):
                        mm = pe.matmul(totals, ones_b[:], hits[:, h, :, c:c + 1].rearrange("p t c -> p (t c)"),
                                       start=(c == 0), stop=(c == GROUP - 1))
                    mm.then_inc(totals_made, 1)

                def rank(h):
                    now = hits[:, h]
                    to = ranks[h % 2].rearrange("p (t c) -> p t c", c=GROUP)
                    if h >= 2 or not isinstance(r, int) or r:
                        pe.wait_ge(masked_made, times(pe, r, BATCHES, h - 1))
                    pe.matmul(to, below_b[:], now, start=True, stop=False)
                    for c in range(GROUP - 1):
                        pe.matmul(to[:, :, c + 1:], ones_b[:],
                                  now[:, :, c:c + 1].to_broadcast([P, NB, GROUP - 1 - c]),
                                  start=False, stop=False)
                    pe.matmul(to, ident_f[:], carry[:, h].unsqueeze(2).to_broadcast([P, NB, GROUP]),
                              start=False, stop=True).then_inc(ranks_made, 1)

                for s in range(STEPS):
                    if t is not None and s == 0:
                        if not isinstance(t, int):
                            pe.wait_ge(xT_kept, t)
                        pe.wait_ge(x_loaded, times(pe, t, 16 * TSLOT, 16 * TSLOT))
                        for q in range(TSLOT):
                            turn(q, P, q == TSLOT - 1)
                    if t is not None and s == 1:
                        pe.wait_ge(xT_kept, plus(pe, t, 1))
                        for q in range(TSLOT):
                            project(q, t, P)
                    if j is not None:
                        if at := lagged(s, 3, j, j1, drain):
                            k, n = at
                            pe.wait_ge(hotT_made[k], n)
                            one_free(pe, qk_made, k, j, n)
                            tile = pe.snap(tile_regs[s], min_val=0, max_val=NT)
                            for b in range(BLK):
                                for a in range(3):
                                    mm = pe.matmul(picked_q[:, b, :], hot_T[:, k, b, :],
                                                   q3[:, bass.ds(tile, 1), a, :].rearrange("p a d -> p (a d)"),
                                                   start=(a == 0), stop=(a == 2))
                            mm.then_inc(q_made[k], 1)
                        if s == BPI - 1 and not drain:
                            next_tiles(pe, tile_regs, j, LQ)
                        if at := lagged(s, 2, j, j1, drain):
                            k, n = at
                            pe.wait_ge(hot_made[k], n)
                            one_free(pe, hotT_made, k, j, n)
                            for b in range(BLK):
                                mm = pe.transpose(turned[:, b, :], hot[:, k, :, b], ident_b[:])
                            mm.then_inc(turned_made[k], 1)
                    if it is not None and s < UNITS:
                        u = s
                        slot_free(pe, rows_kept, u, 1, it, it1)
                        pe.matmul(rows_bank[:], sel,
                                  dst_local[0:ITERS, UNIT * u:UNIT * (u + 1), :].rearrange("p a b -> p (a b)"),
                                  start=True, stop=True).then_inc(spread_rows[u], 1)
                    if it is not None and 2 <= s <= UNITS + 1:
                        u = s - 2
                        pe.wait_ge(pick_made[u], it1)
                        if u % 2 == 0:
                            pe.wait_ge(window_in[u // 2], it16)
                        for n in (2 * u, 2 * u + 1):
                            slot_free(pe, payload_made, n, KVS, it, it1)
                            for k in range(2):
                                to = kv_bank[n % KVS][:, k * 2 * D:(k + 1) * 2 * D]
                                row = (n % 2) * 2 + k
                                for a in range(3):
                                    mm = pe.matmul(to, pick[:, u % 2, row * P:(row + 1) * P],
                                                   window[:, u // 2, a, :], start=(a == 0), stop=(a == 2))
                            mm.then_inc(kv_made[n], 1)
                    if r is not None and s < BATCHES:
                        total(s)
                        rank(s)
                    if j is not None:
                        if at := lagged(s, 5, j, j1, drain):
                            k, n = at
                            pe.wait_ge(msg_made[k], n)
                            one_free(pe, acc_made, k, j, n)
                            for b in range(BLK):
                                mm = pe.matmul(sums, hot_f[:, k, b, :], msg[:, k, b, :],
                                               start=(b == 0), stop=(b == BLK - 1))
                            mm.then_inc(sum_made[k], 1)

            run(pe, before + rows, emit, enter)
            emit(None, JS, None, None, drain=True)

        @block.vector
        def _(dve):
            step = [0]

            def link(ins):
                step[0] += 1
                ins.then_inc(dve_step, 1)
                dve.wait_ge(dve_step, step[0])

            dve.memset(edge_i, NT * P).then_inc(edge_pads, 1)
            dve.memset(dest_i, N - 1).then_inc(edge_pads, 1)
            dve.wait_ge(edges_in, 64)
            dve.tensor_copy(edge_f[0:ITERS], edge_i[0:ITERS]).then_inc(edges_f, 1)
            dve.tensor_copy(dest_f[0:ITERS], dest_i[0:ITERS]).then_inc(edges_f, 1)
            dve.wait_ge(edges_f, 2)
            grouped = dest_f[0:ITERS].rearrange("p (g e) -> p g e", g=GROUPS)
            link(dve.tensor_reduce(span[0:ITERS, 0, :], grouped, AX.X, ALU.min))
            link(dve.tensor_reduce(span[0:ITERS, 1, :], grouped, AX.X, ALU.max))
            link(dve.tensor_copy(span_i[0:ITERS, :], span[0:ITERS, 0, :]))
            link(dve.tensor_tensor(span[0:ITERS, 1, :], span[0:ITERS, 1, :], span[0:ITERS, 0, :], ALU.subtract))
            dve.tensor_reduce(over_f[0:ITERS, :], span[0:ITERS, 1, :], AX.X, ALU.max).then_inc(span_made, 1)

            for n in range(2 * ROWS_IT):
                to, k = (src_i, dst_col)[n // ROWS_IT], n % ROWS_IT
                dve.wait_ge(turned_edges, n + 1)
                dve.tensor_copy(to[:, :, k], turn_ps[n % 2][:, 0:ITERS]).then_inc(kept_edges, 1)
                if n == ROWS_IT:
                    for g in range(GROUPS):
                        dve.tensor_scalar(dst_local[0:ITERS, g * GROUP:(g + 1) * GROUP, :]
                                          .rearrange("p a b -> p (a b)"),
                                          dest_f[0:ITERS, g * GROUP * P:(g + 1) * GROUP * P],
                                          span[0:ITERS, 0, g:g + 1], None, ALU.subtract).then_inc(local_made, 1)
            dve.wait_ge(kept_edges, 2 * ROWS_IT)
            link(dve.tensor_single_scalar(bits_i[:], src_i[:], 7, ALU.logical_shift_right))
            link(dve.tensor_copy(src_tile[:], bits_i[:]))
            link(dve.tensor_single_scalar(bits_i[:], src_i[:], P - 1, ALU.bitwise_and))
            link(dve.tensor_copy(src_node, bits_i[:]))
            dve.wait_ge(base_in, 32)
            link(dve.tensor_reduce(flag_f[:], overs_f[:], AX.X, ALU.max))
            dve.tensor_scalar(flag_i[:], flag_f[:], float(P - 1), None, ALU.is_gt).then_inc(flag_made, 1)
            dve.wait_ge(consts, NCONST)

            def hit(q, row, h):
                dve.tensor_tensor(hits[:, q], src_tile[:, bass.ds(row, 1), h * GROUP:(h + 1) * GROUP]
                                  .to_broadcast([P, NB, GROUP]), tile_row[:], ALU.is_equal).then_inc(hits_made, 1)

            for p in range(NPART):
                first = IT0[p] // 2

                def pair(i, fresh=False):
                    for q in range(2):
                        if not fresh:
                            dve.wait_ge(count_used, dve.snap(i * 2 + (2 * first + q + 1 - 2)))
                        dve.tensor_tensor(
                            hits[:, GROUPS * q:GROUPS * (q + 1)],
                            src_tile[:, bass.ds(i * 2 + (IT0[p] + q), 1), :]
                            .rearrange("p o (g c) -> p (o g) c", g=GROUPS).unsqueeze(2)
                            .to_broadcast([P, GROUPS, NB, GROUP]),
                            tile_row[:].unsqueeze(1).to_broadcast([P, GROUPS, NB, GROUP]),
                            ALU.is_equal).then_inc(hits_made, 2)

                if p == 0:
                    pair(0, fresh=True)
                    with dve.Fori(1, PARTS[p] // 2) as i:
                        pair(i)
                else:
                    with dve.Fori(0, PARTS[p] // 2) as i:
                        pair(i)
                dve.wait_ge(hist_made, p + 1)
                dve.tensor_reduce(count[:, p, :], hist[:, 0:NT * GROUP].rearrange("p (t c) -> p t c", c=GROUP),
                                  AX.X, ALU.add).then_inc(count_made, 1)
            dve.wait_ge(count_made, NPART)
            link(dve.tensor_copy(count_i[:], count[:]))
            link(dve.tensor_single_scalar(count_i[:], count_i[:], 9, ALU.logical_shift_right))
            link(dve.tensor_scalar(blocks_f[:], count_i[:], 1.0, None, ALU.add))
            for p in range(NPART):
                link(dve.tensor_tensor_scan(block_end[:, p, :], one_row[:], blocks_f[:, p, :], 0.0,
                                            ALU.mult, ALU.add))
            for c in range(2 * NPART):
                link(dve.tensor_scalar(cmp_tile[:, c % 2], block_end[:, c // 2, :], node_col[:, c % 2:c % 2 + 1],
                                       None, ALU.is_le))
                ins = dve.tensor_reduce(tile_of[:, c:c + 1], cmp_tile[:, c % 2], AX.X, ALU.add)
                if c < 2 * NPART - 1:
                    link(ins)
            ins.then_inc(tiles_made, 1)
            for p in range(NPART):
                link(dve.tensor_tensor(base[:, p, 0:NT], block_end[:, p, :], blocks_f[:, p, :], ALU.subtract))
                ins = dve.tensor_scalar(base[:, p, 0:NT], base[:, p, 0:NT], float(J0[p] * BPI), float(BROWS),
                                        ALU.add, ALU.mult)
                link(ins)
                link(dve.tensor_scalar(tail_i[0:1, p * NT:(p + 1) * NT], block_end[0:1, p, :],
                                       float(J0[p] * BPI - 1), None, ALU.add))
            dve.wait_ge(tilerow_made, 1)
            for p in range(NPART):
                link(dve.tensor_copy(tile_f[0:1, J0[p] * BPI:(J0[p] + GITERS[p]) * BPI],
                                     tile_ps[p][:, 0:GITERS[p] * BPI]))
            dve.wait_ge(consts, NCONST + 1)
            link(dve.tensor_copy(tile_i[:, 0:NBLK], tile_f[0:1]))
            link(dve.tensor_scalar(live_f[0:1], tile_f[0:1], float(NT), None, ALU.is_lt))
            link(dve.tensor_tensor(start_f[0:1], blk_iota[0:1], live_f[0:1], ALU.mult))
            link(dve.tensor_copy(start_i[:], start_f[0:1]))
            dve.sem_inc(tables_made, 1)

            def first_rest(s, made, n, parts):
                dve.wait_ge(proj_made, made)
                dve.wait_ge(high_made, made)
                dve.tensor_tensor(rest[0:n, s, :], proj_ps[s][0:n, :], parts[0:n, 0, :], ALU.subtract
                                  ).then_inc(split_step, 1)

            def second(s, done, n, parts):
                dve.wait_ge(split_step, done)
                dve.tensor_copy(parts[0:n, 1, :], rest[0:n, s, :]).then_inc(split_step, 1)

            def third(s, done, n, parts):
                dve.wait_ge(split_step, done)
                dve.tensor_tensor(parts[0:n, 2, :], rest[0:n, s, :], parts[0:n, 1, :], ALU.subtract
                                  ).then_inc(low_made, 1)

            LA = BPI
            acc_regs = [dve.alloc_register(f"tile{k}") for k in range(BPI)]

            part = [0]

            def enter(it, j, r, t):
                if it == 0:
                    first_rest(0, FULL_NT + 1, NREST, last3)
                    second(0, 2 * FULL_NT + 1, NREST, last3)
                    third(0, 2 * FULL_NT + 2, NREST, last3)
                if r == 0:
                    for h in range(GROUPS):
                        hit(h, 0, h)
                if r is not None and 2 * r in IT0:
                    part[0] = IT0.index(2 * r)
                    if part[0]:
                        dve.wait_ge(carry_made, BATCHES * r + part[0])
                    dve.tensor_copy(carry[:, 0], base[:, part[0], :]).then_inc(carry_made, 1)

            def emit(it, j, r, t, drain=False):
                if it is not None:
                    it1 = plus(dve, it, 1)
                if j is not None:
                    j1, halves = plus(dve, j, 1), halves_of(dve, j)

                def batch(h):
                    return times(dve, r, 2, h // GROUPS)

                def add_totals(h):
                    dve.wait_ge(totals_made, times(dve, r, BATCHES, h + 1))
                    dve.wait_ge(carry_made, times(dve, r, BATCHES, h + part[0] + 1))
                    dve.tensor_tensor(carry[:, (h + 1) % BATCHES], carry[:, h], totals, ALU.add
                                      ).then_inc(carry_made, 1)

                def mask(h):
                    dve.wait_ge(ranks_made, times(dve, r, BATCHES, h + 1))
                    if h >= 2 or not isinstance(r, int) or r:
                        dve.wait_ge(place_made, times(dve, r, BATCHES, h - 1))
                    dve.tensor_tensor(masked[:, h % 2].rearrange("p t c -> p (t c)"), ranks[h % 2],
                                      hits[:, h].rearrange("p t c -> p (t c)"), ALU.mult).then_inc(masked_made, 1)

                def places(h):
                    g = h % GROUPS
                    dve.wait_ge(masked_made, times(dve, r, BATCHES, h + 1))
                    dve.tensor_reduce(place[:, bass.ds(batch(h), 1), g * GROUP:(g + 1) * GROUP]
                                      .rearrange("p a c -> p (a c)"),
                                      masked[:, h % 2].rearrange("p t c -> p c t"), AX.X, ALU.add
                                      ).then_inc(place_made, 1)

                for s in range(STEPS):
                    if r is not None:
                        if s < 2:
                            hit(s + 2, batch(s + 2), s)
                        if s < BATCHES:
                            add_totals(s)
                    if t is not None:
                        if s == 2:
                            for q in range(TSLOT):
                                first_rest(q, times(dve, t, TSLOT, q + 1), P, parts3[:, q])
                        if s == 3:
                            for q in range(TSLOT):
                                second(q, times(dve, t, 2 * TSLOT, q + 1), P, parts3[:, q])
                        if s == 4:
                            for q in range(TSLOT):
                                third(q, times(dve, t, 2 * TSLOT, TSLOT + q + 1), P, parts3[:, q])
                    if j is not None:
                        if at := lagged(s, LA, j, j1, drain):
                            k, n = at
                            dve.wait_ge(sum_made[k], n)
                            if k:
                                dve.wait_ge(acc_made[k - 1], n)
                            tile = dve.snap(acc_regs[s], min_val=0, max_val=NT)
                            now = acc[:, bass.ds(tile, 1), :].rearrange("p a d -> p (a d)")
                            dve.tensor_tensor(now, now, sums, ALU.add).then_inc(acc_made[k], 1)
                        if s == BPI - 1 and not drain:
                            next_tiles(dve, acc_regs, j, LA)
                    if j is not None and (at := lagged(s, 1, j, j1, drain)):
                        k, n = at
                        dve.wait_ge(tag_made[k], n)
                        dve.tensor_tensor(hot[:, k], tags[:, k, :].unsqueeze(1).to_broadcast([P, P, BLK]),
                                          node_row[:], ALU.is_equal).then_inc(hot_made[k], 1)
                    if j is not None:
                        if at := lagged(s, 4, j, j1, drain):
                            k, n = at
                            dve.wait_ge(score_made, times(dve, j, BPI, k + 1 if s >= 4 else k + 1 - BPI))
                            dve.tensor_scalar(clipped[:, k].rearrange("p b h -> p (b h)"), score[:, k], -CLIP, CLIP,
                                              ALU.max, ALU.min).then_inc(clip_made[k], 1)
                        if at := lagged(s, 3, j, j1, drain):
                            k, n = at
                            dve.wait_ge(q_made[k], n)
                            dve.tensor_tensor(qk[:, k % 2], picked_q, held(k, s < 3, halves, slice(0, D)), ALU.mult
                                              ).then_inc(qk_made[k], 1)
                    if it is not None and 1 <= s <= UNITS:
                        u = s - 1
                        dve.wait_ge(rows_kept[u], it1)
                        slot_free(dve, kv_made[1::2], u, 2, it, it1)
                        dve.tensor_scalar(pick[:, u % 2], dst_rows[:, u % 2], node_col[:, 0:1], None, ALU.is_equal
                                          ).then_inc(pick_made[u], 1)
                    if j is not None:
                        if it is not None and (at := lagged(s, 4, j, j1, drain)):
                            weigh(dve, *at, s < 4, halves)
                        if at := lagged(s, 3, j, j1, drain):
                            k, n = at
                            dve.wait_ge(qk_made[k], n)
                            dve.tensor_reduce(score[:, k], qk[:, k % 2].rearrange("p b (h f) -> p (b h) f", h=HEADS),
                                              AX.X, ALU.add).then_inc(score_made, 1)
                    if r is not None:
                        if 1 <= s <= BATCHES:
                            mask(s - 1)
                        if 2 <= s <= BATCHES + 1:
                            places(s - 2)
                        if s in (3, 4) and not (isinstance(r, int) and r == LAST_PAIR):
                            hit(s - 3, times(dve, r, 2, 2), s - 3)
                if j is not None and not drain and not isinstance(j, int):
                    dve.wait_ge(acc_made[BPI - 1], j)

            run(dve, before + rows, emit, enter)
            emit(None, JS, None, None, drain=True)

            dve.wait_ge(acc_made[BPI - 1], JS)
            link(dve.tensor_scalar(inv, acc[:, 0:NT, D:AW], EPS_W, None, ALU.add))
            link(dve.reciprocal(inv, inv))
            dve.wait_ge(loads, 48 + 32)
            for lo, hi in CHUNKS:
                y = acc[:, lo:hi, 0:D]
                y4 = y.rearrange("p t (h f) -> p t h f", h=HEADS)
                link(dve.tensor_tensor(y4, y4, inv[:, lo:hi].unsqueeze(3).to_broadcast([P, hi - lo, HEADS, DH]),
                                       ALU.mult))
                link(dve.scalar_tensor_tensor(y, x_all[:, lo:hi, :], 2.0, y, ALU.mult, ALU.add))
                link(dve.tensor_reduce(stat[:, 0, lo:hi], y, AX.X, ALU.add))
                link(dve.tensor_scalar(stat[:, 1, lo:hi], stat[:, 0, lo:hi], 1.0 / D, None, ALU.mult))
                dve.tensor_tensor(y, y, stat[:, 1, lo:hi].unsqueeze(2).to_broadcast([P, hi - lo, D]),
                                  ALU.subtract).then_inc(centered, 1)
            for c, (lo, hi) in enumerate(CHUNKS):
                dve.wait_ge(square_made, c + 1)
                link(dve.tensor_reduce(stat[:, 0, lo:hi], sq_all[:, lo:hi, :], AX.X, ALU.add))
            dve.tensor_scalar(stat[:, 2, :], stat[:, 0, :], 1.0 / D, EPS_LN, ALU.mult, ALU.add
                              ).then_inc(centered, 1)
            dve.wait_ge(square_made, len(CHUNKS) + 1)
            link(dve.reciprocal(stat[:, 4, :], stat[:, 3, :]))
            for lo, hi in CHUNKS:
                y = acc[:, lo:hi, 0:D]
                dve.tensor_tensor(y, y, stat[:, 4, lo:hi].unsqueeze(2).to_broadcast([P, hi - lo, D]), ALU.mult
                                  ).then_inc(y_made, 1)


_INS = ["x", "src", "dst", "L0_gnn_qW", "L0_gnn_kW", "L0_gnn_vW"]


def kernel(**inputs):
    import numpy as np
    import concourse.bacc as bacc
    from concourse.bass_utils import run_bass_kernel_spmd

    nc = bacc.Bacc("TRN2", target_bir_lowering=False, num_devices=1)
    arrays, args = {}, []
    for name in _INS:
        a = np.ascontiguousarray(inputs[name])
        arrays[f"in_{name}"] = a
        args.append(nc.dram_tensor(f"in_{name}", a.shape, mybir.dt.from_np(a.dtype), kind="ExternalInput").ap())
    x, src, dst, wq, wk, wv = args
    out = nc.dram_tensor("out", arrays["in_x"].shape, F32, kind="ExternalOutput").ap()
    gnn_program(nc, x, src, dst, wq, wk, wv, out)
    r = run_bass_kernel_spmd(nc, [arrays], core_ids=[0])
    return r.results[0]["out"]
```
